# Optimizing a Trainium2 kernel written in Bass

```python
import numpy as np
import jax
import jax.numpy as jnp

def _softmax(x, axis=-1):
    return jax.nn.softmax(x, axis=axis)

def _gelu(x):
    return jax.nn.gelu(x, approximate=True)

def _silu(x):
    return jax.nn.silu(x)

def _sigmoid(x):
    return jax.nn.sigmoid(x)

def _layernorm(x, axis=-1, eps=1e-05):
    m = jnp.mean(x, axis=axis, keepdims=True)
    v = jnp.var(x, axis=axis, keepdims=True)
    return (x - m) / jnp.sqrt(v + eps)

def _scatter_add(tgt, idx, src, axis=0):
    return tgt.at[idx].add(src)

def _segment_sum(src, seg, n):
    return jax.ops.segment_sum(src, seg, n)
kernel_name = 'mk_perceiver_d1_seqx_r2_feef65'

def setup_inputs(seed: int=0):
    np.random.seed(seed)
    _w = jnp.asarray

    def _rec_inputs():
        import jax
        import jax.numpy as jnp
        _rk = jax.random.key(seed)
        x = -0.0003929 + 0.9999 * jax.random.normal(jax.random.fold_in(_rk, 1), (1, 256, 512), jnp.float32)
        _lenS = 256 - jax.random.randint(jax.random.fold_in(_rk, 7), (1,), 0, max(1, 256 // 4) + 1, jnp.int32)
        _lenS2 = 25088 - jax.random.randint(jax.random.fold_in(_rk, 8), (1,), 0, max(1, 25088 // 4) + 1, jnp.int32)
        _ctx_1024P = jax.random.normal(jax.random.fold_in(_rk, 11), (1, 16, 512), jnp.float32)
        _ctx_1024c = jax.random.dirichlet(jax.random.fold_in(_rk, 511), 0.3 * jnp.ones((16,), jnp.float32), (1, 25088))
        _ctx_1024t = jnp.einsum('bsk,bkd->bsd', _ctx_1024c, _ctx_1024P)
        _ctx_1024t = _ctx_1024t * jax.lax.rsqrt(jnp.mean(jnp.square(_ctx_1024t)) + 1e-12) * 0.953939
        ctx_1024 = 4.13588e-05 + 0.999923 * (_ctx_1024t + 0.3 * jax.random.normal(jax.random.fold_in(_rk, 611), (1, 25088, 512), jnp.float32))
        return (x, ctx_1024)
    x, ctx_1024 = _rec_inputs()

    def _L0_xattn_setup():
        import jax, jax.numpy as jnp
        import numpy as np
        H = 512
        B = 8
        L_CHAR = 1024
        L_SUB = 512

        def _linear(x, W, b):
            return jnp.einsum('blh,oh->blo', x, W) + b

        def _interp_linear(x, out_len):
            L_in = x.shape[1]
            pos = (jnp.arange(out_len, dtype=x.dtype) + 0.5) * (L_in / out_len) - 0.5
            pos = jnp.clip(pos, 0.0, L_in - 1)
            lo = jnp.floor(pos).astype(jnp.int32)
            hi = jnp.minimum(lo + 1, L_in - 1)
            w = (pos - lo.astype(x.dtype))[None, :, None]
            return x[:, lo] * (1 - w) + x[:, hi] * w
        key = jax.random.key(seed)
        ks = jax.random.split(key, 18)
        s = 0.02
        inp = {'char_emb': jax.random.normal(ks[0], (B, L_CHAR, H), jnp.float32), 'subword_emb': jax.random.normal(ks[1], (B, L_SUB, H), jnp.float32)}
        names = ['Wq_c', 'Wk_s', 'Wv_s', 'Wq_s', 'Wk_c', 'Wv_c']
        for i, n in enumerate(names):
            inp[n] = jax.random.normal(ks[2 + 2 * i], (H, H), jnp.float32) * s
            inp['b' + n[1:]] = jax.random.normal(ks[3 + 2 * i], (H,), jnp.float32) * s
        inp['Wg'] = jax.random.normal(ks[14], (H, 2 * H), jnp.float32) * s
        inp['bg'] = jax.random.normal(ks[15], (H,), jnp.float32) * s
        return inp
    _L0_xattn_all = _L0_xattn_setup()
    _L0_xattn_in = {k: v for k, v in _L0_xattn_all.items() if k in ('Wq_c', 'bq_c', 'Wk_s', 'bk_s', 'Wv_s', 'bv_s', 'Wq_s', 'bq_s', 'Wk_c', 'bk_c', 'Wv_c', 'bv_c', 'Wg', 'bg')}
    del _L0_xattn_all

    def _L0_attn_setup():
        import jax, jax.numpy as jnp
        import numpy as np
        D_MODEL, D_K, D_V, N_HEADS = (512, 64, 64, 16)
        BATCH, N_CTX = (2, 1024)

        def half_causal_allowed(n):
            i = jnp.arange(n)[:, None]
            j = jnp.arange(n)[None, :]
            top = (i < n // 2) & (j < n // 2)
            bot = (i >= n // 2) & (j <= i)
            return top | bot
        key = jax.random.key(seed)
        ks = jax.random.split(key, 8)
        s_in = 1.0 / np.sqrt(D_MODEL)
        s_out = 1.0 / np.sqrt(D_V * N_HEADS)
        return {'x': jax.random.normal(ks[0], (BATCH, N_CTX, D_MODEL), jnp.float32), 'Wq': jax.random.uniform(ks[1], (D_MODEL, D_K * N_HEADS), jnp.float32, -s_in, s_in), 'bq': jax.random.uniform(ks[2], (D_K * N_HEADS,), jnp.float32, -s_in, s_in), 'Wk': jax.random.uniform(ks[3], (D_MODEL, D_K * N_HEADS), jnp.float32, -s_in, s_in), 'bk': jax.random.uniform(ks[4], (D_K * N_HEADS,), jnp.float32, -s_in, s_in), 'Wv': jax.random.uniform(ks[5], (D_MODEL, D_V * N_HEADS), jnp.float32, -s_in, s_in), 'bv': jax.random.uniform(ks[6], (D_V * N_HEADS,), jnp.float32, -s_in, s_in), 'Wo': jax.random.uniform(ks[7], (D_V * N_HEADS, D_MODEL), jnp.float32, -s_out, s_out)}
    _L0_attn_all = _L0_attn_setup()
    _L0_attn_in = {k: v for k, v in _L0_attn_all.items() if k in ('Wq', 'bq', 'Wk', 'bk', 'Wv', 'bv', 'Wo')}
    del _L0_attn_all

    def _L0_ffn_setup():
        import jax, jax.numpy as jnp
        import numpy as np
        H = 512
        I = 1024
        E = 32
        B, S = (4, 1024)

        def _grouped_mm(a, w, group_sizes):
            return jax.lax.ragged_dot(a, w, group_sizes)

        def _swiglu(x, gw, uw, dw):
            return jax.nn.silu(x @ gw) * (x @ uw) @ dw
        key = jax.random.key(seed)
        ks = jax.random.split(key, 8)
        scale = 0.02
        inp = {'hidden_states': jax.random.normal(ks[0], (B, S, H), dtype=jnp.float32), 'gate_w': jax.random.normal(ks[1], (H, E), dtype=jnp.float32) * scale, 'shared_gate_w': jax.random.normal(ks[2], (H, I), dtype=jnp.float32) * scale, 'shared_up_w': jax.random.normal(ks[3], (H, I), dtype=jnp.float32) * scale, 'shared_down_w': jax.random.normal(ks[4], (I, H), dtype=jnp.float32) * scale, 'routed_gate_w': jax.random.normal(ks[5], (E, H, I), dtype=jnp.float32) * scale, 'routed_up_w': jax.random.normal(ks[6], (E, H, I), dtype=jnp.float32) * scale, 'routed_down_w': jax.random.normal(ks[7], (E, I, H), dtype=jnp.float32) * scale}
        return inp
    _L0_ffn_all = _L0_ffn_setup()
    _L0_ffn_in = {k: v for k, v in _L0_ffn_all.items() if k in ('gate_w', 'shared_gate_w', 'shared_up_w', 'shared_down_w', 'routed_gate_w', 'routed_up_w', 'routed_down_w')}
    del _L0_ffn_all
    return {'x': x, 'ctx_1024': ctx_1024, 'L0_xattn_Wq_c': _L0_xattn_in['Wq_c'], 'L0_xattn_bq_c': _L0_xattn_in['bq_c'], 'L0_xattn_Wk_s': _L0_xattn_in['Wk_s'], 'L0_xattn_bk_s': _L0_xattn_in['bk_s'], 'L0_xattn_Wv_s': _L0_xattn_in['Wv_s'], 'L0_xattn_bv_s': _L0_xattn_in['bv_s'], 'L0_xattn_Wq_s': _L0_xattn_in['Wq_s'], 'L0_xattn_bq_s': _L0_xattn_in['bq_s'], 'L0_xattn_Wk_c': _L0_xattn_in['Wk_c'], 'L0_xattn_bk_c': _L0_xattn_in['bk_c'], 'L0_xattn_Wv_c': _L0_xattn_in['Wv_c'], 'L0_xattn_bv_c': _L0_xattn_in['bv_c'], 'L0_xattn_Wg': _L0_xattn_in['Wg'], 'L0_xattn_bg': _L0_xattn_in['bg'], 'L0_attn_Wq': _L0_attn_in['Wq'], 'L0_attn_bq': _L0_attn_in['bq'], 'L0_attn_Wk': _L0_attn_in['Wk'], 'L0_attn_bk': _L0_attn_in['bk'], 'L0_attn_Wv': _L0_attn_in['Wv'], 'L0_attn_bv': _L0_attn_in['bv'], 'L0_attn_Wo': _L0_attn_in['Wo'], 'L0_ffn_gate_w': _L0_ffn_in['gate_w'], 'L0_ffn_shared_gate_w': _L0_ffn_in['shared_gate_w'], 'L0_ffn_shared_up_w': _L0_ffn_in['shared_up_w'], 'L0_ffn_shared_down_w': _L0_ffn_in['shared_down_w'], 'L0_ffn_routed_gate_w': _L0_ffn_in['routed_gate_w'], 'L0_ffn_routed_up_w': _L0_ffn_in['routed_up_w'], 'L0_ffn_routed_down_w': _L0_ffn_in['routed_down_w']}

def reference(x, ctx_1024, L0_xattn_Wq_c, L0_xattn_bq_c, L0_xattn_Wk_s, L0_xattn_bk_s, L0_xattn_Wv_s, L0_xattn_bv_s, L0_xattn_Wq_s, L0_xattn_bq_s, L0_xattn_Wk_c, L0_xattn_bk_c, L0_xattn_Wv_c, L0_xattn_bv_c, L0_xattn_Wg, L0_xattn_bg, L0_attn_Wq, L0_attn_bq, L0_attn_Wk, L0_attn_bk, L0_attn_Wv, L0_attn_bv, L0_attn_Wo, L0_ffn_gate_w, L0_ffn_shared_gate_w, L0_ffn_shared_up_w, L0_ffn_shared_down_w, L0_ffn_routed_gate_w, L0_ffn_routed_up_w, L0_ffn_routed_down_w):
    import jax
    import jax.numpy as jnp

    def _L0_xattn_ref(char_emb, subword_emb, Wq_c, bq_c, Wk_s, bk_s, Wv_s, bv_s, Wq_s, bq_s, Wk_c, bk_c, Wv_c, bv_c, Wg, bg):
        import jax, jax.numpy as jnp
        import numpy as np
        H = 512
        B = 8
        L_CHAR = 1024
        L_SUB = 512

        def _linear(x, W, b):
            return jnp.einsum('blh,oh->blo', x, W) + b

        def _interp_linear(x, out_len):
            L_in = x.shape[1]
            pos = (jnp.arange(out_len, dtype=x.dtype) + 0.5) * (L_in / out_len) - 0.5
            pos = jnp.clip(pos, 0.0, L_in - 1)
            lo = jnp.floor(pos).astype(jnp.int32)
            hi = jnp.minimum(lo + 1, L_in - 1)
            w = (pos - lo.astype(x.dtype))[None, :, None]
            return x[:, lo] * (1 - w) + x[:, hi] * w
        h = char_emb.shape[-1]
        scale = 1.0 / jnp.sqrt(jnp.asarray(h, char_emb.dtype))
        Q_char = _linear(char_emb, Wq_c, bq_c)
        K_sub = _linear(subword_emb, Wk_s, bk_s)
        V_sub = _linear(subword_emb, Wv_s, bv_s)
        scores = jnp.einsum('bqh,bkh->bqk', Q_char, K_sub) * scale
        char2sub = jnp.einsum('bqk,bkh->bqh', jax.nn.softmax(scores, axis=-1), V_sub)
        Q_sub = _linear(subword_emb, Wq_s, bq_s)
        K_char = _linear(char_emb, Wk_c, bk_c)
        V_char = _linear(char_emb, Wv_c, bv_c)
        scores2 = jnp.einsum('bqh,bkh->bqk', Q_sub, K_char) * scale
        sub2char = jnp.einsum('bqk,bkh->bqh', jax.nn.softmax(scores2, axis=-1), V_char)
        L_char = char_emb.shape[1]
        if sub2char.shape[1] != L_char:
            sub2char = _interp_linear(sub2char, L_char)
        gate_in = jnp.concatenate([char2sub, sub2char], axis=-1)
        gate = jax.nn.sigmoid(jnp.einsum('blh,oh->blo', gate_in, Wg) + bg)
        return gate * char2sub + (1 - gate) * sub2char

    def _L0_attn_ref(x, Wq, bq, Wk, bk, Wv, bv, Wo):
        import jax, jax.numpy as jnp
        import numpy as np
        D_MODEL, D_K, D_V, N_HEADS = (512, 64, 64, 16)
        BATCH, N_CTX = (2, 1024)

        def half_causal_allowed(n):
            i = jnp.arange(n)[:, None]
            j = jnp.arange(n)[None, :]
            top = (i < n // 2) & (j < n // 2)
            bot = (i >= n // 2) & (j <= i)
            return top | bot
        b, n, _ = x.shape
        h, dk, dv = (N_HEADS, D_K, D_V)
        q = (x @ Wq + bq).reshape(b, n, h, dk).transpose(0, 2, 1, 3)
        k = (x @ Wk + bk).reshape(b, n, h, dk).transpose(0, 2, 1, 3)
        v = (x @ Wv + bv).reshape(b, n, h, dv).transpose(0, 2, 1, 3)
        scores = jnp.einsum('bhqd,bhkd->bhqk', q / jnp.sqrt(jnp.float32(dk)), k)
        allowed = half_causal_allowed(n)
        scores = jnp.where(allowed, scores, -jnp.inf)
        attn = jax.nn.softmax(scores, axis=-1)
        out = jnp.einsum('bhqk,bhkd->bhqd', attn, v)
        out = out.transpose(0, 2, 1, 3).reshape(b, n, h * dv)
        return out @ Wo

    def _L0_ffn_ref(hidden_states, gate_w, shared_gate_w, shared_up_w, shared_down_w, routed_gate_w, routed_up_w, routed_down_w):
        import jax, jax.numpy as jnp
        import numpy as np
        H = 512
        I = 1024
        E = 32
        B, S = (4, 1024)

        def _grouped_mm(a, w, group_sizes):
            return jax.lax.ragged_dot(a, w, group_sizes)

        def _swiglu(x, gw, uw, dw):
            return jax.nn.silu(x @ gw) * (x @ uw) @ dw
        b, s, h = hidden_states.shape
        x = hidden_states.reshape(-1, h)
        shared_out = _swiglu(x, shared_gate_w, shared_up_w, shared_down_w)
        logits = x @ gate_w
        topk_ids = jnp.argmax(logits, axis=-1)
        topk_val = jnp.max(logits, axis=-1)
        scores = jax.nn.sigmoid(topk_val)[:, None]
        xs = x * scores
        tokens_per_expert = jnp.zeros((E,), jnp.int32).at[topk_ids].add(1)
        order = jnp.argsort(topk_ids)
        sorted_x = xs[order]
        g = _grouped_mm(sorted_x, routed_gate_w, tokens_per_expert)
        u = _grouped_mm(sorted_x, routed_up_w, tokens_per_expert)
        d = _grouped_mm(jax.nn.silu(g) * u, routed_down_w, tokens_per_expert)
        inv = jnp.argsort(order)
        routed_out = d[inv]
        return (shared_out + routed_out).reshape(b, s, h)
    x = x + _L0_xattn_ref(_layernorm(x, axis=-1), ctx_1024, L0_xattn_Wq_c, L0_xattn_bq_c, L0_xattn_Wk_s, L0_xattn_bk_s, L0_xattn_Wv_s, L0_xattn_bv_s, L0_xattn_Wq_s, L0_xattn_bq_s, L0_xattn_Wk_c, L0_xattn_bk_c, L0_xattn_Wv_c, L0_xattn_bv_c, L0_xattn_Wg, L0_xattn_bg)
    x = x + _L0_attn_ref(_layernorm(x, axis=-1), L0_attn_Wq, L0_attn_bq, L0_attn_Wk, L0_attn_bk, L0_attn_Wv, L0_attn_bv, L0_attn_Wo)
    x = x + _L0_ffn_ref(_layernorm(x, axis=-1), L0_ffn_gate_w, L0_ffn_shared_gate_w, L0_ffn_shared_up_w, L0_ffn_shared_down_w, L0_ffn_routed_gate_w, L0_ffn_routed_up_w, L0_ffn_routed_down_w)
    return x

_drawn_inputs = setup_inputs


def setup_inputs(seed=0):
    import zlib

    import numpy as np

    out = dict(_drawn_inputs(seed))
    spreads = {}
    factors = {'L0_xattn_Wq_c': 6.737,
     'L0_xattn_bq_c': 8.0,
     'L0_xattn_Wk_s': 6.923,
     'L0_xattn_bk_s': 8.0,
     'L0_xattn_bv_s': 4.925,
     'L0_xattn_Wq_s': 8.0,
     'L0_xattn_bq_s': 8.0,
     'L0_xattn_Wk_c': 8.0,
     'L0_xattn_bk_c': 8.0,
     'L0_xattn_Wv_c': 4.007,
     'L0_xattn_bv_c': 5.114,
     'L0_xattn_Wg': 8.0,
     'L0_xattn_bg': 8.0,
     'L0_attn_Wq': 5.31,
     'L0_attn_bq': 8.0,
     'L0_attn_Wk': 5.319,
     'L0_attn_bk': 8.0,
     'L0_attn_bv': 3.492}
    for name, (base, spread) in spreads.items():
        noise = np.random.default_rng([zlib.crc32(name.encode()), seed]).standard_normal(out[name].shape)
        drawn = base * np.exp(spread * noise) if base else spread * noise
        out[name] = jnp.asarray(drawn.astype(out[name].dtype))
    for name, factor in factors.items():
        out[name] = (out[name] * factor).astype(out[name].dtype)
    return out
```

```python
import concourse.bass as bass
from concourse import mybir
from contextlib import ExitStack

F32 = mybir.dt.float32
F32R = mybir.dt.float32r
BF16 = mybir.dt.bfloat16
I32 = mybir.dt.int32
ACT = mybir.ActivationFunctionType
ALU = mybir.AluOpType
AX_X = mybir.AxisListType.X

P = 128
D = 512
NQ = 256
NK = 25088
HC = D // P
QT = NQ // P
BLK = 512
NB = NK // BLK
KT = BLK // P
NSEL = 2 * NQ
NH = 16
DK = 64
DA = NH * DK
AC = DA // P
HB = 4
E = 32
FI = 1024
IC = FI // P
SLOT = 32
OV = NQ // SLOT - 1
RING = 3
JG = P // SLOT
GW = FI // JG
XSCALE = float(D) ** -0.5
ASCALE = float(DK) ** -0.5
EPS = 1e-5
LOWEST = -3.0e38
MASKED = -1.0e30
assert NB * BLK == NK and NB % 2 == 1 and (E + 1) % RING == 0 and NSEL == HC * P


class Chain:

    def __init__(self, eng, sem):
        self.eng, self.sem, self.n, self.i, self.per = eng, sem, 0, None, 0

    def __call__(self, ins):
        self.n += 1
        ins.then_inc(self.sem, 1)
        self.eng.wait_ge(self.sem, self.n if self.i is None else self.i * self.per + self.n)

    def enter(self, i, per):
        self.i, self.per, self.mark = i, per, self.n

    def leave(self, trips):
        assert self.n - self.mark == self.per, self.n - self.mark
        self.n, self.i = self.mark + self.per * trips, None


def perceiver_layer(nc, a):
    with ExitStack() as ctx:
        LOW = 16512
        RINGB = 81888
        WB = D * FI * 4 // P

        def at(name, shape, dt, offset):
            return nc.alloc_sbuf_tensor_at(name, shape, dt, offset=offset)

        cursor = [LOW]

        def place(name, shape, dt=F32):
            size = 4 if dt in (F32, F32R, I32) else 2
            for s in shape[1:]:
                size *= s
            t = at(name, shape, dt, cursor[0])
            cursor[0] += (size + 31) // 32 * 32
            assert cursor[0] <= RINGB, (name, cursor[0])
            return t

        ident = place("ident", [P, P])
        identb = place("identb", [P, P], BF16)
        maskb = place("maskb", [P, P], BF16)
        ones = place("ones", [P, P])
        upper = place("upper", [P, P])
        iota32i = place("iota32i", [P, SLOT], I32)
        iota32 = place("iota32", [P, SLOT])
        slot_tab_i = place("slot_tab_i", [P, E + OV], I32)
        slot_tab = place("slot_tab", [P, E + OV])
        x = place("x", [P, QT, D])
        cols = place("cols", [P, 32])
        st = place("st", [P, 100])
        w_router = place("w_router", [P, HC, E])
        small = cursor[0]
        rows = place("rows", [P, 5 * D])
        shared_low = cursor[0]

        acc = place("acc", [P, QT, D])
        pexp = place("pexp", [P, QT, BLK])
        pt_hi = place("pt_hi", [P, QT, KT, P], F32R)
        pt_lo = place("pt_lo", [P, QT, KT, P], F32R)
        q_hi = place("q_hi", [P, HC, NQ], F32R)
        q_lo = place("q_lo", [P, HC, NQ], F32R)
        s2c = place("s2c", [P, QT, D])
        gate2 = place("gate2", [P, QT, D])
        w_gate2 = place("w_gate2", [P, HC, D])
        w_gate1 = at("w_gate1", [P, HC, D], F32, cursor[0] - HC * D * 4)
        acc_t = at("acc_t", [P, HC, NQ], F32, shared_low + 1 * 4096)
        c2s = at("c2s", [P, QT, D], F32, shared_low + 2 * 4096)
        c2s_t = at("c2s_t", [P, HC, NQ], F32, shared_low + 3 * 4096)
        gate = at("gate", [P, QT, D], F32, shared_low + 4 * 4096)
        accn = at("accn", [P, QT, D], F32, shared_low + 5 * 4096)

        cursor[0] = shared_low
        an = place("an", [P, QT, D])
        a_t = place("a_t", [P, HC, NQ])
        qpad = place("qpad", [P, AC, 2, NQ])
        k_t = place("k_t", [P, AC, NQ])
        va = place("va", [P, QT, DA])

        cursor[0] = small
        y = place("y", [P, QT, D])
        y_t = place("y_t", [P, HC, NQ])
        gsel = place("gsel", [P, QT, E, SLOT])
        gsel_ov = place("gsel_ov", [P, QT, OV, SLOT])
        xg_all = place("xg_all", [P, HC, (E + OV) * SLOT])
        h_t = place("h_t", [P, IC, NQ])
        slot_row = place("slot_row", [P, NQ])
        xg = place("xg", [P, HC, SLOT])
        sg = place("sg", [P, GW])
        hh = place("hh", [P, GW])
        hh_t = place("hh_t", [P, 2, P])
        dd = place("dd", [P, D])
        scat_at = cursor[0]
        scat = place("scat", [P, NQ])
        slot_rep = at("slot_rep", [P, QT, P], F32, scat_at)
        cmp = at("cmp", [P, E, OV], F32, small + 4096 * 2 + 8192)
        eo_i = place("eo_i", [P, 8], I32)
        logits = place("logits", [P, QT, E])
        onehot = place("onehot", [P, QT, E])
        rank_hot = place("rank_hot", [P, QT, E])
        iota_m = place("iota_m", [P, E])
        counts, extra, before, upto0, upto1 = (place(n, [P, E])[:, :] for n in
                                               ("counts", "extra", "before", "upto0", "upto1"))
        pre = [upto0, upto1]
        thr = place("thr", [P, OV])[:, :]
        eo = place("eo", [P, OV + 1])[:, :]
        tsel = place("tsel", [P, QT, OV])[:, :, :]
        tok = place("tok", [P, 10 * QT])
        maxlog, tscale, eidm, rank, passes, tile_no, rem, is_more, s_first, s_more = (
            tok[:, k * QT:(k + 1) * QT] for k in range(10))

        kb = HC * BLK * 4
        nat = [at(f"nat{k}", [P, KT, D], F32, RINGB + k * kb) for k in range(2)]
        ctt = [at(f"ctt{k}", [P, HC, BLK], F32, RINGB + (2 + k) * kb) for k in range(2)]
        nat_hi = [at(f"nat_hi{k}", [P, KT, D], F32R, RINGB + (4 + k) * kb) for k in range(2)]
        nat_lo = [at(f"nat_lo{k}", [P, KT, D], F32R, RINGB + (6 + k) * kb) for k in range(2)]
        ctt_hi = [at(f"ctt_hi{k}", [P, HC, BLK], F32R, RINGB + (8 + k) * kb) for k in range(2)]
        ctt_lo = [at(f"ctt_lo{k}", [P, HC, BLK], F32R, RINGB + (10 + k) * kb) for k in range(2)]
        o = RINGB + 5 * kb
        xn = at("xn", [P, QT, D], F32, o)
        c_t = at("c_t", [P, HC, NQ], F32, o + 4096)
        o = RINGB + 7 * kb
        qc_t = at("qc_t", [P, HC, NQ], F32, o)
        kc_t = at("kc_t", [P, HC, NQ], F32, o + 4096)
        o = RINGB + 9 * kb
        kq_t = at("kq_t", [P, HC, NQ], F32, o)
        vc = at("vc", [P, QT, D], F32, o + 4096)
        o = RINGB + 11 * kb
        sc2 = at("sc2", [P, 4, NQ], F32, o)
        s2c_t = at("s2c_t", [P, HC, NQ], F32, o + 4096)
        o = RINGB + 4 * kb
        pavg = at("pavg", [P, QT, NQ], F32, o)
        pavg_t = at("pavg_t", [P, QT, NQ], F32, o + 2048)
        bias2 = at("bias2", [P, NQ], F32, o + 4096)
        bqs_rep = at("bqs_rep", [P, HC, P], F32, o + 5120)
        o = RINGB + 12 * kb
        w_qc, w_ks, w_kc, w_qs, w_vc, sel_t = (at(n, [P, HC, D], F32, o + k * kb) for k, n in
                                              enumerate(("w_qc", "w_ks", "w_kc", "w_qs", "w_vc", "sel_t")))
        w_vs = at("w_vs", [P, HC, D], F32, RINGB + 3 * kb)
        w_q = at("w_q", [P, HC, DA], F32, RINGB + 2 * 3 * WB)
        w_k = at("w_k", [P, HC, DA], F32, RINGB + (2 * 3 + 1) * WB)
        w_v = at("w_v", [P, HC, DA], F32, RINGB + (2 * 3 + 2) * WB)
        w_o = at("w_o", [P, AC, D], F32, RINGB + 2 * 3 * WB)
        o_t = at("o_t", [P, AC, NQ], F32, RINGB + (2 * 3 + 1) * WB)
        patt = at("patt", [P, HB, 384], F32, RINGB + (2 * 3 + 1) * WB + 8192)
        patt_t = at("patt_t", [P, 2, 384], F32, RINGB + (2 * 3 + 2) * WB)
        wg = [at(f"wg{k}", [P, HC, FI], F32, RINGB + 3 * k * WB) for k in range(RING)]
        wu = [at(f"wu{k}", [P, HC, FI], F32, RINGB + (3 * k + 1) * WB) for k in range(RING)]
        wd = [at(f"wd{k}", [P, IC, D], F32, RINGB + (3 * k + 2) * WB) for k in range(RING)]

        ps = ctx.enter_context(nc.psum_tensor("ps", [P, 8, 512], F32))

        def bank(k, n=1):
            return ps[:, k, :] if n == 1 else ps[:, k:k + n, :]

        b_qc, b_kc, b_ks, b_qs = cols[:, 0:4], cols[:, 4:8], cols[:, 8:12], cols[:, 12:16]
        b_q, b_k = cols[:, 16:24], cols[:, 24:32]
        r_vc, r_vs, r_g, r_v = rows[:, 0:D], rows[:, D:2 * D], rows[:, 2 * D:3 * D], rows[:, 3 * D:5 * D]

        names = """
        x_loaded cols_loaded rows_loaded wqc_loaded wks_loaded wkc_loaded wqs_loaded wvc_loaded sel_loaded
        wg2_loaded wg1_loaded wvs_loaded nat_loaded0 nat_loaded1 ctt_loaded0 ctt_loaded1 watt_loaded wo_loaded
        gw_loaded0 gw_loaded1 gw_loaded2 uw_loaded0 uw_loaded1 uw_loaded2 dw_loaded0 dw_loaded1 dw_loaded2
        wr_loaded out_stored
        consts_made pool_step dve_step act_step
        var_ready sd_ready
        xn_ready ct_in_psum ct_lo_ready ct_hi_ready qc_in_psum qc_ready kc_in_psum kc_ready qk_in_psum cb_in_psum
        qhi_ready qlo_ready rep_ready bias2_in_psum bias2_ready kq_in_psum kq_ready vc_in_psum vc_ready
        sc2_in_psum sc2_taken neg2_ready p2_ready pavg_ready pavgt_in_psum pavgt_ready s2ct_in_psum s2ct_ready
        s2c_in_psum s2c_ready gate2_in_psum gate2_ready
        nat_hi_ready nat_lo_ready ctt_hi_ready ctt_lo_ready scores_ready bias_ready exp_ready alpha_ready
        pt_in_psum pt_hi_ready pt_lo_ready pv_in_psum acc_ready
        accn_ready acct_in_psum acct_ready c2s_in_psum c2s_ready c2st_in_psum c2st_ready gate1_in_psum z_ready
        gate_ready an_ready at_in_psum at_ready qpad_zero qa_in_psum qa_evac_act qa_evac_dve ka_in_psum ka_ready
        va_in_psum va_ready
        as_in_psum abias_ready aexp_ready aprob_ready apt_in_psum apt_ready aot_in_psum aot_ready ao_in_psum
        y_ready yt_in_psum yt_ready logits_in_psum maxlog_ready token_scale_ready onehot_ready ranks_in_psum
        sh_gate_in_psum sh_up_in_psum sh_silu_ready sh_h_ready sh_down_done
        gsel_ready gather_in_psum gather_ready slotrep_ready slotrow_in_psum slotrow_ready
        xg_ready gate_done silu_ready up_done h_ready ht_in_psum ht_ready down_done d_ready scat_ready
        scatter_done overflow_known out_ready
        """.split()
        s = {n: ctx.enter_context(nc.semaphore(n)) for n in names}
        nat_loaded = [s["nat_loaded0"], s["nat_loaded1"]]
        ctt_loaded = [s["ctt_loaded0"], s["ctt_loaded1"]]
        gw_loaded = [s["gw_loaded0"], s["gw_loaded1"], s["gw_loaded2"]]
        uw_loaded = [s["uw_loaded0"], s["uw_loaded1"], s["uw_loaded2"]]
        dw_loaded = [s["dw_loaded0"], s["dw_loaded1"], s["dw_loaded2"]]

        def cell(k, n=1):
            return st[:, k:k + n]

        stats, mv, rstd = cell(0, 12), cell(12, 4), cell(16, 2)
        cb, mrun, nbias, dmax = cell(18, 2), [cell(20, 2), cell(22, 2)], [cell(24, 2), cell(26, 2)], cell(28, 2)
        bmax, alpha, rsum, lrun = cell(30, 2), [cell(32, 2), cell(34, 2)], [cell(36, 2), cell(38, 2)], cell(40, 2)
        lrec, max2, neg2, sum2, rec2 = cell(42, 2), cell(44, 4), cell(48, 4), cell(52, 4), cell(80, 4)
        amax, aneg, asum, arec = ([cell(k + 2 * m, 2) for m in range(HB)] for k in (60, 68, 84, 92))
        var, sd, newt = cell(76, 2), cell(78, 2), cell(58, 2)

        block = ctx.enter_context(nc.Block())

        head_bank = [6, 7, 2, 3]

        def chunks(w, n=P):
            return w.rearrange("(c p) n -> p c n", p=n)

        @block.sync
        def _(sp):
            sp.dma_start(x[:, :, :], a["x"].rearrange("a (t p) d -> p (a t) d", p=P)).then_inc(s["x_loaded"], 16)
            sp.dma_start(cols[:, :], a["bias_cols"]).then_inc(s["cols_loaded"], 16)
            sp.dma_start(w_router[:, :, :], chunks(a["w_router"])).then_inc(s["wr_loaded"], 16)
            for dst, src, sem in ((w_qc, a["w_qc_t"], s["wqc_loaded"]), (w_kc, a["w_kc_t"], s["wkc_loaded"]),
                                  (w_ks, a["w_ks"], s["wks_loaded"]), (w_qs, a["w_qs"], s["wqs_loaded"])):
                sp.dma_start(dst[:, :, :], chunks(src)).then_inc(sem, 16)
            sp.dma_start(rows[:, :], a["bias_rows"].partition_broadcast(P)).then_inc(s["rows_loaded"], 16)

            def load_block(b, par):
                first = b * BLK
                sp.dma_start(ctt[par][:, :, :], chunks(a["ctx_t"])[:, :, bass.ds(first, BLK)]).then_inc(ctt_loaded[par], 16)
                sp.dma_start(nat[par][:, :, :], a["ctx_rows"][bass.ds(first, BLK), :].rearrange("(t p) d -> p t d", p=P)
                             ).then_inc(nat_loaded[par], 16)

            sp.dma_start(w_vc[:, :, :], chunks(a["w_vc_t"])).then_inc(s["wvc_loaded"], 16)
            sp.dma_start(sel_t[:, :, :], chunks(a["sel_t"])).then_inc(s["sel_loaded"], 16)
            load_block(0, 0)
            sp.dma_start(w_gate2[:, :, :], chunks(a["w_g_t"][D:2 * D, :])).then_inc(s["wg2_loaded"], 16)
            load_block(1, 1)
            sp.wait_ge(s["gate2_in_psum"], 1)
            sp.dma_start(w_gate1[:, :, :], chunks(a["w_g_t"][0:D, :])).then_inc(s["wg1_loaded"], 16)
            sp.dma_start(w_k[:, :, :], chunks(a["w_k"])).then_inc(s["watt_loaded"], 16)
            sp.dma_start(w_v[:, :, :], chunks(a["w_v"])).then_inc(s["watt_loaded"], 16)
            sp.dma_start(w_q[:, :, :], chunks(a["w_q"])).then_inc(s["watt_loaded"], 16)

            def next_block(b, par):
                sp.wait_ge(s["ctt_hi_ready"], b - 1)
                sp.wait_ge(s["ctt_lo_ready"], b - 1)
                sp.wait_ge(s["nat_hi_ready"], b - 1)
                sp.wait_ge(s["nat_lo_ready"], b - 1)
                load_block(b, par)

            with sp.Fori(0, (NB - 3) // 2) as i:
                next_block(i * 2 + 2, 0)
                next_block(i * 2 + 3, 1)
            next_block(NB - 1, 0)
            sp.wait_ge(s["ctt_hi_ready"], NB - 1)
            sp.wait_ge(s["ctt_lo_ready"], NB - 1)
            sp.dma_start(w_vs[:, :, :], chunks(a["w_vs_t"])).then_inc(s["wvs_loaded"], 16)

            def load_expert(k, g, u, d):
                sp.dma_start(wg[k][:, :, :], g).then_inc(gw_loaded[k], 16)
                sp.dma_start(wu[k][:, :, :], u).then_inc(uw_loaded[k], 16)
                sp.dma_start(wd[k][:, :, :], d).then_inc(dw_loaded[k], 16)

            def expert_weights(e):
                return (a["r_gate"][bass.ds(e, 1)].rearrange("a (c p) n -> p (a c) n", p=P),
                        a["r_up"][bass.ds(e, 1)].rearrange("a (c p) n -> p (a c) n", p=P),
                        a["r_down"][bass.ds(e, 1)].rearrange("a (c p) n -> p (a c) n", p=P))

            sp.wait_ge(s["c2s_in_psum"], 1)
            load_expert(0, chunks(a["s_gate"]), chunks(a["s_up"]), chunks(a["s_down"]))
            load_expert(1, *expert_weights(0))
            sp.wait_ge(s["qa_in_psum"], AC)
            sp.dma_start(w_o[:, :, :], chunks(a["w_o"])).then_inc(s["wo_loaded"], 16)
            sp.wait_ge(s["ao_in_psum"], 2)
            load_expert(2, *expert_weights(1))

            def next_expert(e, k):
                g, u, d = expert_weights(e)
                sp.wait_ge(s["gate_done"], e - 2)
                sp.dma_start(wg[k][:, :, :], g).then_inc(gw_loaded[k], 16)
                sp.wait_ge(s["up_done"], e - 2)
                sp.dma_start(wu[k][:, :, :], u).then_inc(uw_loaded[k], 16)
                sp.wait_ge(s["down_done"], e - 2)
                sp.dma_start(wd[k][:, :, :], d).then_inc(dw_loaded[k], 16)

            g2, u2, d2 = expert_weights(2)
            sp.wait_ge(s["sh_gate_in_psum"], IC)
            sp.dma_start(wg[0][:, :, :], g2).then_inc(gw_loaded[0], 16)
            next_expert(3, 1)
            next_expert(4, 2)
            sp.wait_ge(s["sh_up_in_psum"], IC)
            sp.dma_start(wu[0][:, :, :], u2).then_inc(uw_loaded[0], 16)
            sp.wait_ge(s["sh_down_done"], 1)
            sp.dma_start(wd[0][:, :, :], d2).then_inc(dw_loaded[0], 16)
            with sp.Fori(1, (E - 2) // RING) as g:
                for k in range(RING):
                    next_expert(g * RING + 2 + k, k)

            sp.wait_ge(s["overflow_known"], 1)
            more = sp.value_load(eo_i[0:1, 7:8], min_val=0, max_val=OV)
            with sp.If(more > 0):
                with sp.Fori(0, OV) as o:
                    e = sp.value_load(eo_i[0:1, bass.ds(o, 1)], min_val=0, max_val=E - 1)
                    sp.wait_ge(s["down_done"], o + E)
                    g_w, u_w, d_w = expert_weights(e)
                    sp.dma_start(wg[0][:, :, :], g_w).then_inc(gw_loaded[0], 16)
                    sp.dma_start(wu[0][:, :, :], u_w).then_inc(uw_loaded[0], 16)
                    sp.dma_start(wd[0][:, :, :], d_w).then_inc(dw_loaded[0], 16)
            for t in range(QT):
                sp.wait_ge(s["out_ready"], t + 1)
                sp.dma_start(a["out"].rearrange("a (t p) d -> p (a t) d", p=P)[:, t, :], x[:, t, :]).then_inc(s["out_stored"], 16)
            sp.wait_ge(s["out_stored"], 32)

        @block.gpsimd
        def _(pool):
            step = Chain(pool, s["pool_step"])
            step(pool.memset(ident[:, :], 0.0))
            step(pool.affine_select(out=ident[:, :], in_=ident[:, :], compare_op=ALU.not_equal, fill=1.0, base=0,
                                    pattern=[[-1, P]], channel_multiplier=1))
            step(pool.memset(identb[:, :], 0.0))
            step(pool.affine_select(out=identb[:, :], in_=identb[:, :], compare_op=ALU.not_equal, fill=1.0, base=0,
                                    pattern=[[-1, P]], channel_multiplier=1))
            step(pool.memset(maskb[:, :], 0.0))
            step(pool.affine_select(out=maskb[:, :], in_=maskb[:, :], compare_op=ALU.is_ge, fill=MASKED, base=0,
                                    pattern=[[-1, P]], channel_multiplier=1))
            step(pool.memset(ones[:, :], 1.0))
            step(pool.memset(upper[:, :], 1.0))
            step(pool.affine_select(out=upper[:, :], in_=upper[:, :], compare_op=ALU.is_gt, fill=0.0, base=0,
                                    pattern=[[1, P]], channel_multiplier=-1))
            step(pool.iota(iota32i[:, :], pattern=[[1, SLOT]], base=0, channel_multiplier=0))
            step(pool.tensor_copy(iota32[:, :], iota32i[:, :]))
            for j in range(JG):
                step(pool.iota(slot_tab_i[j * SLOT:(j + 1) * SLOT, :], pattern=[[SLOT, E + OV]], base=0,
                               channel_multiplier=1))
            pool.tensor_copy(slot_tab[:, :], slot_tab_i[:, :]).then_inc(s["consts_made"], 1)
            pool.wait_ge(s["an_ready"], QT)
            pool.wait_ge(s["gate1_in_psum"], 1)
            pool.memset(qpad[:, :, :, :], 0.0).then_inc(s["qpad_zero"], 1)

        @block.tensor
        def _(pe):
            mm = pe.matmul

            def transposes(src, dst, sem, rows_n=QT, cols_n=HC):
                for t in range(rows_n):
                    for c in range(cols_n):
                        last = pe.transpose(dst[:, c, t * P:(t + 1) * P], src[:, t, c * P:(c + 1) * P], ident[:, :])
                last.then_inc(sem, 1)

            def by_chunk(k, n=HC):
                return ps[:, k:k + n // 2, :].rearrange("p b (h n) -> p (b h) n", n=NQ)

            def weight_stationary(out, w, act, n_out, sem, per=False):
                for o in range(n_out):
                    for c in range(HC):
                        last = mm(out[:, o, :], w[:, c, o * P:(o + 1) * P], act[:, c, :], start=(c == 0), stop=(c == HC - 1))
                    if per:
                        last.then_inc(sem, 1)
                if not per:
                    last.then_inc(sem, 1)

            def scores(b, par):
                pe.wait_ge(s["ctt_hi_ready"], b + 1)
                pe.wait_ge(s["ctt_lo_ready"], b + 1)
                for q in range(QT):
                    for c in range(HC):
                        qh, ql = q_hi[:, c, q * P:(q + 1) * P], q_lo[:, c, q * P:(q + 1) * P]
                        o = ps[:, 2 * (1 - par) + q, :]
                        mm(o, qh, ctt_hi[par][:, c, :], start=(c == 0), stop=False)
                        mm(o, qh, ctt_lo[par][:, c, :], start=False, stop=False)
                        last = mm(o, ql, ctt_hi[par][:, c, :], start=False, stop=(c == HC - 1))
                last.then_inc(s["scores_ready"], 1)

            def transpose_probs(b):
                pe.wait_ge(s["exp_ready"], b + 1)
                for q in range(QT):
                    for t in range(KT):
                        last = pe.transpose(ps[:, 4 + q, t * P:(t + 1) * P], pexp[:, q, t * P:(t + 1) * P], ident[:, :])
                last.then_inc(s["pt_in_psum"], 1)

            def products(b, par):
                pe.wait_ge(s["nat_hi_ready"], b + 1)
                pe.wait_ge(s["nat_lo_ready"], b + 1)
                pe.wait_ge(s["pt_hi_ready"], b + 1)
                pe.wait_ge(s["pt_lo_ready"], b + 1)
                pe.wait_ge(s["acc_ready"], b + 1)
                for q in range(QT):
                    for t in range(KT):
                        o = ps[:, 6 + q, :]
                        mm(o, pt_hi[:, q, t, :], nat_hi[par][:, t, :], start=(t == 0), stop=False)
                        mm(o, pt_hi[:, q, t, :], nat_lo[par][:, t, :], start=False, stop=False)
                        last = mm(o, pt_lo[:, q, t, :], nat_hi[par][:, t, :], start=False, stop=(t == KT - 1))
                last.then_inc(s["pv_in_psum"], 1)

            pe.wait_ge(s["consts_made"], 1)
            pe.wait_ge(s["xn_ready"], QT)
            transposes(xn, by_chunk(0), s["ct_in_psum"])
            pe.wait_ge(s["ct_lo_ready"], 1)
            pe.wait_ge(s["ct_hi_ready"], 1)
            pe.wait_ge(s["wqc_loaded"], 16)
            weight_stationary(by_chunk(2), w_qc, c_t, HC, s["qc_in_psum"])
            pe.wait_ge(s["wkc_loaded"], 16)
            weight_stationary(by_chunk(4), w_kc, c_t, HC, s["kc_in_psum"])
            pe.wait_ge(s["qc_ready"], 1)
            pe.wait_ge(s["wks_loaded"], 16)
            weight_stationary(by_chunk(6), w_ks, qc_t, HC, s["qk_in_psum"])
            pe.wait_ge(s["cols_loaded"], 16)
            for t in range(QT):
                for c in range(HC):
                    last = mm(ps[:, 0, t:t + 1], qc_t[:, c, t * P:(t + 1) * P], b_ks[:, c:c + 1],
                              start=(c == 0), stop=(c == HC - 1))
            last.then_inc(s["cb_in_psum"], 1)
            pe.wait_ge(s["kc_ready"], 1)
            pe.wait_ge(s["wqs_loaded"], 16)
            weight_stationary(by_chunk(2), w_qs, kc_t, HC, s["kq_in_psum"])
            pe.wait_ge(s["rep_ready"], 1)
            for c in range(HC):
                last = mm(ps[:, 1, 0:NQ], bqs_rep[:, c, :], kc_t[:, c, :], start=(c == 0), stop=(c == HC - 1))
            last.then_inc(s["bias2_in_psum"], 1)
            pe.wait_ge(s["wvc_loaded"], 16)
            for t in range(QT):
                for c in range(HC):
                    last = mm(ps[:, 4 + t, :], c_t[:, c, t * P:(t + 1) * P], w_vc[:, c, :], start=(c == 0), stop=(c == HC - 1))
            last.then_inc(s["vc_in_psum"], 1)
            pe.wait_ge(s["kq_ready"], 1)
            pe.wait_ge(s["bias2_ready"], 1)
            pe.wait_ge(s["qlo_ready"], 1)
            pe.wait_ge(s["sel_loaded"], 16)
            out = by_chunk(0)
            for t in range(NSEL // P):
                for c in range(HC):
                    last = mm(out[:, t, :], sel_t[:, c, t * P:(t + 1) * P], kq_t[:, c, :], start=(c == 0), stop=(c == HC - 1))
            last.then_inc(s["sc2_in_psum"], 1)
            scores(0, 0)
            pe.wait_ge(s["pavg_ready"], 1)
            pe.wait_ge(s["vc_ready"], 1)
            transposes(pavg, ps[:, 4, :].rearrange("p (c n) -> p c n", n=NQ), s["pavgt_in_psum"], QT, QT)
            pe.wait_ge(s["pavgt_ready"], 1)
            out = by_chunk(0)
            for o in range(HC):
                for c in range(QT):
                    last = mm(out[:, o, :], vc[:, c, o * P:(o + 1) * P], pavg_t[:, c, :], start=(c == 0), stop=(c == QT - 1))
            last.then_inc(s["s2ct_in_psum"], 1)
            for t in range(QT):
                for c in range(QT):
                    last = mm(ps[:, 6 + t, :], pavg_t[:, c, t * P:(t + 1) * P], vc[:, c, :], start=(c == 0), stop=(c == QT - 1))
            last.then_inc(s["s2c_in_psum"], 1)
            transpose_probs(0)
            pe.wait_ge(s["s2ct_ready"], 1)
            pe.wait_ge(s["wg2_loaded"], 16)
            for t in range(QT):
                for c in range(HC):
                    last = mm(ps[:, 2 + t, :], s2c_t[:, c, t * P:(t + 1) * P], w_gate2[:, c, :], start=(c == 0), stop=(c == HC - 1))
            last.then_inc(s["gate2_in_psum"], 1)

            pe.wait_ge(s["s2c_ready"], 1)
            pe.wait_ge(s["gate2_ready"], 1)
            with pe.Fori(0, (NB - 1) // 2) as i:
                for par in (1, 0):
                    b = i * 2 + (1 if par else 2)
                    scores(b, par)
                    products(b - 1, 1 - par)
                    transpose_probs(b)
            products(NB - 1, 0)

            pe.wait_ge(s["accn_ready"], 1)
            transposes(accn, by_chunk(0), s["acct_in_psum"])
            pe.wait_ge(s["acct_ready"], 2)
            pe.wait_ge(s["wvs_loaded"], 16)
            for t in range(QT):
                for c in range(HC):
                    last = mm(ps[:, 2 + t, :], acc_t[:, c, t * P:(t + 1) * P], w_vs[:, c, :], start=(c == 0), stop=(c == HC - 1))
            last.then_inc(s["c2s_in_psum"], 1)
            pe.wait_ge(s["c2s_ready"], 1)
            transposes(c2s, by_chunk(4), s["c2st_in_psum"])
            pe.wait_ge(s["c2st_ready"], 2)
            pe.wait_ge(s["wg1_loaded"], 16)
            for t in range(QT):
                for c in range(HC):
                    last = mm(ps[:, 6 + t, :], c2s_t[:, c, t * P:(t + 1) * P], w_gate1[:, c, :], start=(c == 0), stop=(c == HC - 1))
            last.then_inc(s["gate1_in_psum"], 1)

            pe.wait_ge(s["an_ready"], QT)
            transposes(an, by_chunk(0), s["at_in_psum"])
            pe.wait_ge(s["at_ready"], 2)
            pe.wait_ge(s["watt_loaded"], 48)
            weight_stationary(by_chunk(2, AC), w_q, a_t, AC, s["qa_in_psum"], per=True)
            k_bank = [6, 6, 7, 7, 0, 0, 1, 1]
            for o in range(AC):
                for c in range(HC):
                    last = mm(ps[:, k_bank[o], (o % 2) * NQ:(o % 2 + 1) * NQ], w_k[:, c, o * P:(o + 1) * P], a_t[:, c, :],
                              start=(c == 0), stop=(c == HC - 1))
                last.then_inc(s["ka_in_psum"], 1)
            pe.wait_ge(s["qa_evac_act"], AC)
            pe.wait_ge(s["qa_evac_dve"], AC)
            for t in range(QT):
                for n in range(2):
                    for c in range(HC):
                        last = mm(ps[:, 2 + 2 * t + n, :], a_t[:, c, t * P:(t + 1) * P], w_v[:, c, n * D:(n + 1) * D],
                                  start=(c == 0), stop=(c == HC - 1))
                    last.then_inc(s["va_in_psum"], 1)

            def head_scores(h):
                c, half, o = h // 2, h % 2, ps[:, head_bank[h % HB], :]
                if h >= HB:
                    pe.wait_ge(s["aexp_ready"], h - HB + 1)
                mm(o[:, 0:P], qpad[:, c, half, 0:P], k_t[:, c, 0:P], start=True, stop=True)
                mm(o[:, P:2 * P], qpad[:, c, half, P:2 * P], k_t[:, c, 0:P], start=True, stop=True)
                mm(o[:, 2 * P:3 * P], qpad[:, c, half, P:2 * P], k_t[:, c, P:2 * P], start=True, stop=False)
                mm(o[:, 2 * P:3 * P], identb[:, :], maskb[:, :], start=False, stop=True).then_inc(s["as_in_psum"], 1)

            def head_transposes(h):
                pe.wait_ge(s["aprob_ready"], h + 1)
                for k in range(3):
                    last = pe.transpose(ps[:, h % 2, k * P:(k + 1) * P], patt[:, h % HB, k * P:(k + 1) * P], ident[:, :])
                last.then_inc(s["apt_in_psum"], 1)

            def head_products(h):
                c, half = h // 2, h % 2
                pe.wait_ge(s["apt_ready"], h + 1)
                if half == 0 and c >= 2:
                    pe.wait_ge(s["aot_ready"], c - 1)
                o = ps[DK * half:DK * (half + 1), 4 + c % 2, :]
                va0, va1 = (va[:, t, h * DK:(h + 1) * DK] for t in range(QT))
                mm(o[:, 0:P], va0, patt_t[:, h % 2, 0:P], start=True, stop=True)
                mm(o[:, P:NQ], va0, patt_t[:, h % 2, P:2 * P], start=True, stop=False)
                last = mm(o[:, P:NQ], va1, patt_t[:, h % 2, 2 * P:3 * P], start=False, stop=True)
                if half:
                    last.then_inc(s["aot_in_psum"], 1)

            pe.wait_ge(s["ka_ready"], AC)
            pe.wait_ge(s["va_ready"], 4)
            for h in range(HB - 1):
                head_scores(h)
            for h in range(NH):
                head_transposes(h)
                if h + HB - 1 < NH:
                    head_scores(h + HB - 1)
                if h:
                    head_products(h - 1)
            head_products(NH - 1)
            pe.wait_ge(s["aot_ready"], AC)
            pe.wait_ge(s["wo_loaded"], 16)
            for t in range(QT):
                for c in range(AC):
                    last = mm(ps[:, 2 + t, :], o_t[:, c, t * P:(t + 1) * P], w_o[:, c, :], start=(c == 0), stop=(c == AC - 1))
                last.then_inc(s["ao_in_psum"], 1)

            pe.wait_ge(s["y_ready"], QT)
            transposes(y, by_chunk(0), s["yt_in_psum"])
            pe.wait_ge(s["yt_ready"], 2)
            pe.wait_ge(s["wr_loaded"], 16)
            for t in range(QT):
                for c in range(HC):
                    last = mm(ps[:, 6, t * E:(t + 1) * E], y_t[:, c, t * P:(t + 1) * P], w_router[:, c, :],
                              start=(c == 0), stop=(c == HC - 1))
            last.then_inc(s["logits_in_psum"], 1)
            pe.wait_ge(gw_loaded[0], 16)
            for i in range(IC):
                if i >= 4:
                    pe.wait_ge(s["sh_silu_ready"], i - 3)
                for c in range(HC):
                    last = mm(ps[:, i % 4, 0:NQ], wg[0][:, c, i * P:(i + 1) * P], y_t[:, c, :], start=(c == 0), stop=(c == HC - 1))
                last.then_inc(s["sh_gate_in_psum"], 1)
                if i == 1:
                    pe.wait_ge(s["onehot_ready"], 1)
                    mm(ps[:, 6, 64:96], upper[:, :], onehot[:, 0, :], start=True, stop=True)
                    mm(ps[:, 6, 96:128], ones[:, :], onehot[:, 0, :], start=True, stop=False)
                    mm(ps[:, 6, 96:128], upper[:, :], onehot[:, 1, :], start=False, stop=True)
                    mm(ps[:, 6, 128:160], ones[:, :], onehot[:, 0, :], start=True, stop=False)
                    mm(ps[:, 6, 128:160], ones[:, :], onehot[:, 1, :], start=False, stop=True).then_inc(s["ranks_in_psum"], 1)
                if i == IC - 2:
                    pe.wait_ge(s["slotrep_ready"], 1)
                    for t in range(QT):
                        last_t = pe.transpose(ps[:, 7, t * P:(t + 1) * P], slot_rep[:, t, :], ident[:, :])
                    last_t.then_inc(s["slotrow_in_psum"], 1)

            def tokens_to_slots(half):
                src_all = gsel_ov if half == 2 else gsel[:, :, half * 16:(half + 1) * 16, :]
                pe.wait_ge(s["gsel_ready"], half + 1)
                for c in range(HC):
                    for t in range(QT):
                        src = src_all[:, t, :, :].rearrange("p e s -> p (e s)")
                        last = mm(ps[:, c, 0:src.shape[1]], y[:, t, c * P:(c + 1) * P], src, start=(t == 0), stop=(t == QT - 1))
                    last.then_inc(s["gather_in_psum"], 1)

            pe.wait_ge(s["sh_silu_ready"], IC)
            tokens_to_slots(0)

            def expert(n, k, rnd, first=False):
                pe.wait_ge(s["xg_ready"], n + 1)
                pe.wait_ge(gw_loaded[k], rnd)
                for c in range(HC):
                    for j in range(JG):
                        last = mm(ps[j * SLOT:(j + 1) * SLOT, 0, 0:GW], xg[:, c, :], wg[k][:, c, j * GW:(j + 1) * GW],
                                  start=(c == 0), stop=(c == HC - 1))
                last.then_inc(s["gate_done"], 1)
                pe.wait_ge(uw_loaded[k], rnd)
                for c in range(HC):
                    for j in range(JG):
                        last = mm(ps[j * SLOT:(j + 1) * SLOT, 1, 0:GW], xg[:, c, :], wu[k][:, c, j * GW:(j + 1) * GW],
                                  start=(c == 0), stop=(c == HC - 1))
                last.then_inc(s["up_done"], 1)
                pe.wait_ge(s["h_ready"], n + 1)
                for m in range(2):
                    last = pe.transpose(ps[:, 2, m * P:(m + 1) * P], hh[:, m * P:(m + 1) * P], ident[:, :])
                last.then_inc(s["ht_in_psum"], 1)
                pe.wait_ge(s["ht_ready"], n + 1)
                pe.wait_ge(dw_loaded[k], rnd)
                for m in range(2):
                    for j in range(JG):
                        last = mm(ps[j * SLOT:(j + 1) * SLOT, 3, :], hh_t[:, m, j * SLOT:(j + 1) * SLOT],
                                  wd[k][:, 2 * j + m, :], start=(m == 0), stop=(m == 1))
                last.then_inc(s["down_done"], 1)
                pe.wait_ge(s["d_ready"], n + 1)
                pe.wait_ge(s["scat_ready"], n + 1)
                for t in range(QT):
                    last = mm(ps[:, 4 + t, :], scat[:, t * P:(t + 1) * P], dd[:, :], start=first, stop=True,
                              skip_group_check=True)
                last.then_inc(s["scatter_done"], 1)

            pe.wait_ge(s["gather_ready"], HC)
            expert(0, 1, 16, first=True)
            expert(1, 2, 16)
            pe.wait_ge(s["h_ready"], 2)
            pe.wait_ge(s["d_ready"], 2)
            pe.wait_ge(s["ht_ready"], 2)
            pe.wait_ge(s["silu_ready"], 2)
            pe.wait_ge(uw_loaded[0], 16)
            for i in range(IC):
                if i >= 4:
                    pe.wait_ge(s["sh_h_ready"], i - 3)
                for c in range(HC):
                    last = mm(ps[:, i % 4, 0:NQ], wu[0][:, c, i * P:(i + 1) * P], y_t[:, c, :], start=(c == 0), stop=(c == HC - 1))
                last.then_inc(s["sh_up_in_psum"], 1)
            pe.wait_ge(dw_loaded[0], 16)
            for i in range(IC):
                pe.wait_ge(s["sh_h_ready"], i + 1)
                for t in range(QT):
                    last = mm(ps[:, 4 + t, :], h_t[:, i, t * P:(t + 1) * P], wd[0][:, i, :], start=False, stop=True,
                              skip_group_check=True)
            last.then_inc(s["sh_down_done"], 1)
            tokens_to_slots(1)
            pe.wait_ge(s["gather_ready"], 2 * HC)
            with pe.Fori(0, (E - 2) // RING) as g:
                for k in range(RING):
                    expert(g * RING + 2 + k, k, g * 16 + 32)
            pe.wait_ge(s["overflow_known"], 1)
            more = pe.value_load(eo_i[0:1, 7:8], min_val=0, max_val=OV)
            with pe.If(more > 0):
                tokens_to_slots(2)
                pe.wait_ge(s["gather_ready"], 3 * HC)
                with pe.Fori(0, OV) as o:
                    expert(o + E, 0, o * 16 + 16 * ((E - 2) // RING + 2))

        @block.scalar
        def _(act):
            step = Chain(act, s["act_step"])

            def deviation(k):
                act.wait_ge(s["var_ready"], k + 1)
                act.activation(sd, var, ACT.Sqrt).then_inc(s["sd_ready"], 1)

            def columns_hi(b, par, sixteens):
                act.wait_ge(ctt_loaded[par], sixteens)
                act.activation(ctt_hi[par][:, :, :], ctt[par][:, :, :], ACT.Copy).then_inc(s["ctt_hi_ready"], 1)

            def rows_hi(b, par, sixteens):
                act.wait_ge(nat_loaded[par], sixteens)
                act.activation(nat_hi[par][:, :, :], nat[par][:, :, :], ACT.Copy).then_inc(s["nat_hi_ready"], 1)

            def probs_hi(b):
                act.wait_ge(s["pt_in_psum"], b + 1)
                act.activation(pt_hi[:, :, :, :].rearrange("p q t n -> p q (t n)"), bank(4, 2), ACT.Copy
                               ).then_inc(s["pt_hi_ready"], 1)

            def exps(b, par):
                act.wait_ge(s["bias_ready"], b + 1)
                for q in range(QT):
                    last = act.activation(pexp[:, q, :], ps[:, 2 * (1 - par) + q, :], ACT.Exp, bias=nbias[par][:, q:q + 1],
                                          accum_out=rsum[par][:, q:q + 1])
                last.then_inc(s["exp_ready"], 1)
                act.activation(alpha[par], dmax, ACT.Exp).then_inc(s["alpha_ready"], 1)

            def two_blocks(i, last=False):
                for par in (1, 0):
                    b = i * 2 + (1 if par else 2)
                    probs_hi(b - 1)
                    rows_hi(b, par, i * 16 + (16 if par else 32))
                    if par or not last:
                        columns_hi(b + 1, 1 - par, i * 16 + 32)
                    exps(b, par)

            deviation(0)
            act.wait_ge(s["ct_in_psum"], 1)
            act.activation(c_t[:, 2:4, :], ps[:, 1, :].rearrange("p (c n) -> p c n", n=NQ), ACT.Copy).then_inc(s["ct_hi_ready"], 1)
            act.wait_ge(s["cols_loaded"], 16)
            act.wait_ge(s["kc_in_psum"], 1)
            for c in range(HC):
                last = act.activation(kc_t[:, c, :], ps[:, 4 + c // 2, (c % 2) * NQ:(c % 2 + 1) * NQ], ACT.Identity,
                                      bias=b_kc[:, c:c + 1])
            last.then_inc(s["kc_ready"], 1)
            act.wait_ge(s["qk_in_psum"], 1)
            act.activation(q_hi[:, :, :], bank(6, 2).rearrange("p b (h n) -> p (b h) n", n=NQ), ACT.Copy,
                           scale=XSCALE).then_inc(s["qhi_ready"], 1)
            act.wait_ge(s["kq_in_psum"], 1)
            act.activation(kq_t[:, :, :], bank(2, 2).rearrange("p b (h n) -> p (b h) n", n=NQ), ACT.Copy).then_inc(s["kq_ready"], 1)
            columns_hi(0, 0, 16)
            act.wait_ge(s["neg2_ready"], 1)
            for t in range(4):
                last = act.activation(sc2[:, t, :], sc2[:, t, :], ACT.Exp, bias=neg2[:, t:t + 1], scale=XSCALE,
                                      accum_out=sum2[:, t:t + 1])
            last.then_inc(s["p2_ready"], 1)
            act.wait_ge(s["pavgt_in_psum"], 1)
            act.activation(pavg_t[:, :, :], ps[:, 4, :].rearrange("p (c n) -> p c n", n=NQ), ACT.Copy).then_inc(s["pavgt_ready"], 1)
            exps(0, 0)
            act.wait_ge(s["s2c_in_psum"], 1)
            act.activation(s2c[:, :, :], bank(6, 2), ACT.Copy).then_inc(s["s2c_ready"], 1)

            act.wait_ge(s["gate2_in_psum"], 1)
            columns_hi(1, 1, 16)
            rows_hi(0, 0, 16)
            with act.Fori(0, (NB - 1) // 2 - 1) as i:
                two_blocks(i)
            two_blocks((NB - 1) // 2 - 1, last=True)
            probs_hi(NB - 1)

            act.wait_ge(s["acct_in_psum"], 1)
            act.activation(acc_t[:, 0:2, :], ps[:, 0, :].rearrange("p (c n) -> p c n", n=NQ), ACT.Copy).then_inc(s["acct_ready"], 1)
            act.wait_ge(s["c2st_in_psum"], 1)
            act.activation(c2s_t[:, 0:2, :], ps[:, 4, :].rearrange("p (c n) -> p c n", n=NQ), ACT.Copy).then_inc(s["c2st_ready"], 1)
            act.wait_ge(s["z_ready"], 1)
            act.activation(gate[:, :, :], gate[:, :, :], ACT.Sigmoid).then_inc(s["gate_ready"], 1)

            deviation(1)
            act.wait_ge(s["at_in_psum"], 1)
            act.activation(a_t[:, 0:2, :], ps[:, 0, :].rearrange("p (c n) -> p c n", n=NQ), ACT.Copy).then_inc(s["at_ready"], 1)
            act.wait_ge(s["qpad_zero"], 1)
            for o in range(AC):
                act.wait_ge(s["qa_in_psum"], o // 2 * 2 + 2)
                act.activation(qpad[0:DK, o, 0, :], ps[0:DK, 2 + o // 2, (o % 2) * NQ:(o % 2 + 1) * NQ], ACT.Identity,
                               bias=b_q[0:DK, o:o + 1]).then_inc(s["qa_evac_act"], 1)
                act.activation(qpad[DK:P, o, 1, :], ps[DK:P, 2 + o // 2, (o % 2) * NQ:(o % 2 + 1) * NQ], ACT.Identity,
                               bias=b_q[DK:P, o:o + 1]).then_inc(s["qa_evac_dve"], 1)
            for h in range(NH):
                act.wait_ge(s["abias_ready"], h + 1)
                o, m = ps[:, head_bank[h % HB], :], h % HB
                act.activation(patt[:, m, 0:P], o[:, 0:P], ACT.Exp, bias=aneg[m][:, 0:1], scale=ASCALE,
                               accum_out=asum[m][:, 0:1])
                act.activation(patt[:, m, P:3 * P], o[:, P:3 * P], ACT.Exp, bias=aneg[m][:, 1:2], scale=ASCALE,
                               accum_out=asum[m][:, 1:2]).then_inc(s["aexp_ready"], 1)
                if h >= 1:
                    act.wait_ge(s["apt_in_psum"], h)
                    act.activation(patt_t[:, (h - 1) % 2, :], ps[:, (h - 1) % 2, 0:3 * P], ACT.Copy).then_inc(s["apt_ready"], 1)
            act.wait_ge(s["apt_in_psum"], NH)
            act.activation(patt_t[:, 1, :], ps[:, 1, 0:3 * P], ACT.Copy).then_inc(s["apt_ready"], 1)

            deviation(2)
            act.wait_ge(s["yt_in_psum"], 1)
            act.activation(y_t[:, 0:2, :], ps[:, 0, :].rearrange("p (c n) -> p c n", n=NQ), ACT.Copy).then_inc(s["yt_ready"], 1)
            act.wait_ge(s["maxlog_ready"], 1)
            act.activation(tscale, maxlog, ACT.Sigmoid).then_inc(s["token_scale_ready"], 1)
            for i in range(IC):
                act.wait_ge(s["sh_gate_in_psum"], i + 1)
                act.activation(h_t[:, i, :], ps[:, i % 4, 0:NQ], ACT.Silu).then_inc(s["sh_silu_ready"], 1)
            def slots_out(half):
                w = OV * SLOT if half == 2 else 512
                for c in range(HC):
                    act.wait_ge(s["gather_in_psum"], half * HC + c + 1)
                    act.activation(xg_all[:, c, half * 512:half * 512 + w], ps[:, c, 0:w], ACT.Copy).then_inc(s["gather_ready"], 1)
                act.wait_ge(s["gather_ready"], (half + 1) * HC)

            def gather(n):
                act.activation(xg[:, :, :], xg_all[:, :, bass.ds(n * SLOT, SLOT)], ACT.Copy).then_inc(s["xg_ready"], 1)

            def expert(n, more=True):
                act.wait_ge(s["gate_done"], n + 1)
                act.activation(sg[:, :], ps[:, 0, 0:GW], ACT.Silu).then_inc(s["silu_ready"], 1)
                act.wait_ge(s["ht_in_psum"], n + 1)
                act.activation(hh_t[:, :, :].rearrange("p m n -> p (m n)"), ps[:, 2, 0:2 * P], ACT.Copy).then_inc(s["ht_ready"], 1)
                if more:
                    gather(n + 1)

            slots_out(0)
            gather(0)
            expert(0)
            expert(1)
            slots_out(1)
            with act.Fori(0, (E - 2) // RING - 1) as g:
                for k in range(RING):
                    expert(g * RING + 2 + k)
            for n in range(E - RING, E):
                expert(n, more=(n < E - 1))
            act.wait_ge(s["overflow_known"], 1)
            more = act.value_load(eo_i[0:1, 7:8], min_val=0, max_val=OV)
            with act.If(more > 0):
                slots_out(2)
                gather(E)
                with act.Fori(0, OV - 1) as o:
                    expert(o + E)
                expert(E + OV - 1, more=False)

        @block.vector
        def _(dve):
            step = Chain(dve, s["dve_step"])

            def layernorm(k, dst, ready):
                for t in range(QT):
                    last = dve.bn_stats(stats[:, 6 * t:6 * t + 6], x[:, t, :])
                step(last)
                for t in range(QT):
                    last = dve.bn_aggr(mv[:, 2 * t:2 * t + 2], stats[:, 6 * t:6 * t + 6])
                step(last)
                dve.tensor_scalar(var, mv[:, 1:4:2], EPS, None, ALU.add).then_inc(s["var_ready"], 1)
                dve.wait_ge(s["sd_ready"], k + 1)
                step(dve.reciprocal(rstd, sd))
                step(dve.tensor_tensor(newt, rstd, rstd, ALU.mult))
                step(dve.tensor_tensor(newt, newt, var, ALU.mult))
                step(dve.tensor_scalar(newt, newt, -0.5, 1.5, ALU.mult, ALU.add))
                step(dve.tensor_tensor(rstd, rstd, newt, ALU.mult))
                for t in range(QT):
                    dve.tensor_scalar(dst[:, t, :], x[:, t, :], mv[:, 2 * t:2 * t + 1], rstd[:, t:t + 1],
                                      ALU.subtract, ALU.mult).then_inc(ready, 1)
                dve.wait_ge(ready, QT)

            def columns_lo(b, par):
                dve.wait_ge(s["ctt_hi_ready"], b + 1)
                dve.tensor_tensor(ctt_lo[par][:, :, :], ctt[par][:, :, :], ctt_hi[par][:, :, :].bitcast(F32),
                                  ALU.subtract).then_inc(s["ctt_lo_ready"], 1)

            def rows_lo(b, par):
                dve.wait_ge(s["nat_hi_ready"], b + 1)
                dve.tensor_tensor(nat_lo[par][:, :, :], nat[par][:, :, :], nat_hi[par][:, :, :].bitcast(F32),
                                  ALU.subtract).then_inc(s["nat_lo_ready"], 1)

            def probs_lo(b):
                dve.wait_ge(s["pt_hi_ready"], b + 1)
                dve.tensor_tensor(pt_lo[:, :, :, :].rearrange("p q t n -> p q (t n)"), bank(4, 2),
                                  pt_hi[:, :, :, :].rearrange("p q t n -> p q (t n)").bitcast(F32),
                                  ALU.subtract).then_inc(s["pt_lo_ready"], 1)

            def block_max(b, par):
                dve.wait_ge(s["scores_ready"], b + 1)
                step(dve.reduce_max(bmax, bank(2 * (1 - par), 2), AX_X))
                step(dve.tensor_tensor(bmax, bmax, cb, ALU.add))
                step(dve.tensor_tensor(mrun[par], mrun[1 - par], bmax, ALU.max))
                dve.tensor_tensor(nbias[par], cb, mrun[par], ALU.subtract)
                dve.tensor_tensor(dmax, mrun[1 - par], mrun[par], ALU.subtract).then_inc(s["bias_ready"], 1)

            def accumulate(b, par):
                dve.wait_ge(s["pv_in_psum"], b + 1)
                dve.wait_ge(s["alpha_ready"], b + 1)
                for q in range(QT):
                    dve.scalar_tensor_tensor(acc[:, q, :], acc[:, q, :], alpha[par][:, q:q + 1], ps[:, 6 + q, :],
                                             ALU.mult, ALU.add)
                step(dve.tensor_tensor(lrun, lrun, alpha[par], ALU.mult))
                dve.tensor_tensor(lrun, lrun, rsum[par], ALU.add).then_inc(s["acc_ready"], 1)
                dve.wait_ge(s["acc_ready"], b + 2)

            dve.wait_ge(s["x_loaded"], 16)
            layernorm(0, xn, s["xn_ready"])
            dve.wait_ge(s["ct_in_psum"], 1)
            dve.tensor_copy(c_t[:, 0:2, :], ps[:, 0, :].rearrange("p (c n) -> p c n", n=NQ)).then_inc(s["ct_lo_ready"], 1)
            dve.wait_ge(s["cols_loaded"], 16)
            dve.wait_ge(s["consts_made"], 1)
            for c in range(HC):
                last = dve.tensor_scalar(bqs_rep[:, c, :], ones[:, :], b_qs[:, c:c + 1], None, ALU.mult)
            last.then_inc(s["rep_ready"], 1)
            dve.wait_ge(s["qc_in_psum"], 1)
            for c in range(HC):
                last = dve.tensor_scalar(qc_t[:, c, :], ps[:, 2 + c // 2, (c % 2) * NQ:(c % 2 + 1) * NQ], b_qc[:, c:c + 1],
                                         None, ALU.add)
            last.then_inc(s["qc_ready"], 1)
            dve.wait_ge(s["qhi_ready"], 1)
            dve.wait_ge(s["cb_in_psum"], 1)
            step(dve.tensor_scalar(cb, ps[:, 0, 0:2], XSCALE, None, ALU.mult))
            dve.scalar_tensor_tensor(q_lo[:, :, :].rearrange("p c n -> p (c n)"), bank(6, 2).rearrange("p b n -> p (b n)"),
                                     XSCALE, q_hi[:, :, :].bitcast(F32).rearrange("p c n -> p (c n)"),
                                     ALU.mult, ALU.subtract).then_inc(s["qlo_ready"], 1)
            dve.wait_ge(s["bias2_in_psum"], 1)
            dve.tensor_copy(bias2[:, :], ps[:, 1, 0:NQ]).then_inc(s["bias2_ready"], 1)
            dve.wait_ge(s["rows_loaded"], 16)
            dve.wait_ge(s["vc_in_psum"], 1)
            for t in range(QT):
                last = dve.tensor_tensor(vc[:, t, :], ps[:, 4 + t, :], r_vc, ALU.add)
            last.then_inc(s["vc_ready"], 1)
            columns_lo(0, 0)
            dve.wait_ge(s["sc2_in_psum"], 1)
            dve.wait_ge(s["bias2_ready"], 1)
            for t in range(4):
                last = dve.tensor_tensor(sc2[:, t, :], ps[:, t // 2, (t % 2) * NQ:(t % 2 + 1) * NQ], bias2[:, :], ALU.add)
            last.then_inc(s["sc2_taken"], 1)
            dve.wait_ge(s["sc2_taken"], 1)
            step(dve.reduce_max(max2, sc2[:, :, :], AX_X))
            dve.tensor_scalar(neg2, max2, -XSCALE, None, ALU.mult).then_inc(s["neg2_ready"], 1)
            dve.wait_ge(s["p2_ready"], 1)
            step(dve.reciprocal(rec2, sum2))
            step(dve.tensor_scalar(rec2, rec2, 0.5, None, ALU.mult))
            for t in range(QT):
                step(dve.tensor_scalar(pavg[:, t, :], sc2[:, 2 + t, :], rec2[:, 2 + t:3 + t], None, ALU.mult))
                last = dve.scalar_tensor_tensor(pavg[:, t, :], sc2[:, t, :], rec2[:, t:t + 1], pavg[:, t, :], ALU.mult, ALU.add)
            last.then_inc(s["pavg_ready"], 1)
            dve.memset(lrun, 0.0)
            step(dve.memset(mrun[1], LOWEST))
            block_max(0, 0)
            dve.wait_ge(s["s2ct_in_psum"], 1)
            dve.tensor_copy(s2c_t[:, :, :], bank(0, 2).rearrange("p b (h n) -> p (b h) n", n=NQ)).then_inc(s["s2ct_ready"], 1)
            dve.memset(acc[:, :, :], 0.0).then_inc(s["acc_ready"], 1)
            dve.wait_ge(s["acc_ready"], 1)

            dve.wait_ge(s["gate2_in_psum"], 1)
            for t in range(QT):
                last = dve.tensor_tensor(gate2[:, t, :], ps[:, 2 + t, :], r_g, ALU.add)
            last.then_inc(s["gate2_ready"], 1)
            columns_lo(1, 1)
            rows_lo(0, 0)

            def two_blocks(i, last=False):
                for par in (1, 0):
                    b = i * 2 + (1 if par else 2)
                    probs_lo(b - 1)
                    rows_lo(b, par)
                    dve.wait_ge(s["alpha_ready"], b)
                    block_max(b, par)
                    if par or not last:
                        columns_lo(b + 1, 1 - par)
                    accumulate(b - 1, 1 - par)

            with dve.Fori(0, (NB - 1) // 2 - 1) as i:
                step.enter(i, 8)
                two_blocks(i)
            step.leave((NB - 1) // 2 - 1)
            two_blocks((NB - 1) // 2 - 1, last=True)
            probs_lo(NB - 1)
            accumulate(NB - 1, 0)

            step(dve.reciprocal(lrec, lrun))
            for q in range(QT):
                last = dve.tensor_scalar(accn[:, q, :], acc[:, q, :], lrec[:, q:q + 1], None, ALU.mult)
            last.then_inc(s["accn_ready"], 1)
            dve.wait_ge(s["acct_in_psum"], 1)
            dve.tensor_copy(acc_t[:, 2:4, :], ps[:, 1, :].rearrange("p (c n) -> p c n", n=NQ)).then_inc(s["acct_ready"], 1)
            dve.wait_ge(s["c2s_in_psum"], 1)
            for t in range(QT):
                last = dve.tensor_tensor(c2s[:, t, :], ps[:, 2 + t, :], r_vs, ALU.add)
            last.then_inc(s["c2s_ready"], 1)
            dve.wait_ge(s["c2st_in_psum"], 1)
            dve.tensor_copy(c2s_t[:, 2:4, :], ps[:, 5, :].rearrange("p (c n) -> p c n", n=NQ)).then_inc(s["c2st_ready"], 1)
            step(dve.tensor_tensor(x[:, :, :], x[:, :, :], s2c[:, :, :], ALU.add))
            step(dve.tensor_tensor(c2s[:, :, :], c2s[:, :, :], s2c[:, :, :], ALU.subtract))
            dve.wait_ge(s["gate1_in_psum"], 1)
            dve.tensor_tensor(gate[:, :, :], bank(6, 2), gate2[:, :, :], ALU.add).then_inc(s["z_ready"], 1)
            dve.wait_ge(s["gate_ready"], 1)
            step(dve.tensor_tensor(c2s[:, :, :], c2s[:, :, :], gate[:, :, :], ALU.mult))
            step(dve.tensor_tensor(x[:, :, :], x[:, :, :], c2s[:, :, :], ALU.add))

            layernorm(1, an, s["an_ready"])
            dve.wait_ge(s["at_in_psum"], 1)
            dve.tensor_copy(a_t[:, 2:4, :], ps[:, 1, :].rearrange("p (c n) -> p c n", n=NQ)).then_inc(s["at_ready"], 1)
            k_bank = [6, 6, 7, 7, 0, 0, 1, 1]
            for o in range(AC):
                dve.wait_ge(s["ka_in_psum"], o // 2 * 2 + 2)
                dve.tensor_scalar(k_t[:, o, :], ps[:, k_bank[o], (o % 2) * NQ:(o % 2 + 1) * NQ], b_k[:, o:o + 1], None,
                                  ALU.add).then_inc(s["ka_ready"], 1)
            for n in range(4):
                dve.wait_ge(s["va_in_psum"], n + 1)
                dve.tensor_tensor(va[:, n // 2, (n % 2) * D:(n % 2 + 1) * D], ps[:, 2 + n, :], r_v[:, (n % 2) * D:(n % 2 + 1) * D],
                                  ALU.add).then_inc(s["va_ready"], 1)

            def head_max(h):
                m, o = h % HB, ps[:, head_bank[h % HB], :]
                dve.wait_ge(s["as_in_psum"], h + 1)
                dve.reduce_max(amax[m][:, 0:1], o[:, 0:P], AX_X)
                step(dve.reduce_max(amax[m][:, 1:2], o[:, P:3 * P], AX_X))
                dve.tensor_scalar(aneg[m], amax[m], -ASCALE, None, ALU.mult).then_inc(s["abias_ready"], 1)

            def head_norm(h):
                m = h % HB
                dve.wait_ge(s["aexp_ready"], h + 1)
                step(dve.reciprocal(arec[m], asum[m]))
                dve.tensor_scalar(patt[:, m, 0:P], patt[:, m, 0:P], arec[m][:, 0:1], None, ALU.mult)
                dve.tensor_scalar(patt[:, m, P:3 * P], patt[:, m, P:3 * P], arec[m][:, 1:2], None, ALU.mult
                                  ).then_inc(s["aprob_ready"], 1)

            def pair_out(c):
                dve.wait_ge(s["aot_in_psum"], c + 1)
                dve.tensor_copy(o_t[:, c, :], ps[:, 4 + c % 2, 0:NQ]).then_inc(s["aot_ready"], 1)

            head_max(0)
            head_max(1)
            for h in range(NH):
                if h + 2 < NH:
                    head_max(h + 2)
                head_norm(h)
                if h >= 4 and h % 2 == 0:
                    pair_out((h - 4) // 2)
            pair_out(AC - 2)
            pair_out(AC - 1)
            for t in range(QT):
                dve.wait_ge(s["ao_in_psum"], t + 1)
                step(dve.tensor_tensor(x[:, t, :], x[:, t, :], ps[:, 2 + t, :], ALU.add))

            layernorm(2, y, s["y_ready"])
            dve.wait_ge(s["yt_in_psum"], 1)
            dve.tensor_copy(y_t[:, 2:4, :], ps[:, 1, :].rearrange("p (c n) -> p c n", n=NQ)).then_inc(s["yt_ready"], 1)

            dve.wait_ge(s["logits_in_psum"], 1)
            step(dve.tensor_copy(logits[:, :, :], ps[:, 6, 0:QT * E].rearrange("p (t e) -> p t e", e=E)))
            dve.reduce_max(maxlog, logits[:, :, :], AX_X).then_inc(s["maxlog_ready"], 1)
            dve.wait_ge(s["maxlog_ready"], 1)
            wide = [P, QT, E]
            step(dve.tensor_tensor(onehot[:, :, :], logits[:, :, :], maxlog.unsqueeze(2).to_broadcast(wide), ALU.is_equal))
            step(dve.tensor_scalar(iota_m[:, :], iota32[:, :], float(-E), None, ALU.add))
            step(dve.tensor_tensor(logits[:, :, :], onehot[:, :, :], iota_m[:, :].unsqueeze(1).to_broadcast(wide), ALU.mult))
            step(dve.tensor_reduce(eidm, logits[:, :, :], axis=AX_X, op=ALU.min))
            dve.tensor_tensor(onehot[:, :, :], iota_m[:, :].unsqueeze(1).to_broadcast(wide),
                              eidm.unsqueeze(2).to_broadcast(wide), ALU.is_equal).then_inc(s["onehot_ready"], 1)
            dve.wait_ge(s["token_scale_ready"], 1)
            dve.wait_ge(s["onehot_ready"], 1)
            for t in range(QT):
                step(dve.tensor_scalar(y[:, t, :], y[:, t, :], tscale[:, t:t + 1], None, ALU.mult))
            dve.wait_ge(s["ranks_in_psum"], 1)
            step(dve.tensor_tensor(logits[:, :, :], ps[:, 6, 64:128].rearrange("p (t e) -> p t e", e=E), onehot[:, :, :], ALU.mult))
            step(dve.tensor_reduce(rank, logits[:, :, :], axis=AX_X, op=ALU.add))
            step(dve.tensor_tensor(rank_hot[:, :, :], iota32[:, :].unsqueeze(1).to_broadcast(wide),
                                   rank.unsqueeze(2).to_broadcast(wide), ALU.is_equal))

            def selection(half):
                for t in range(QT):
                    last = dve.tensor_tensor(gsel[:, t, half * 16:(half + 1) * 16, :],
                                             onehot[:, t, half * 16:(half + 1) * 16].unsqueeze(2).to_broadcast([P, 16, SLOT]),
                                             rank_hot[:, t, :].unsqueeze(1).to_broadcast([P, 16, SLOT]), ALU.mult)
                last.then_inc(s["gsel_ready"], 1)

            step(dve.tensor_scalar(thr, iota32[:, 0:OV], float(SLOT), float(SLOT), ALU.mult, ALU.add))
            ew = [P, E, OV]
            step(dve.tensor_copy(counts, ps[:, 6, 128:160]))
            step(dve.tensor_tensor(cmp[:, :, :], counts.unsqueeze(2).to_broadcast(ew), thr.unsqueeze(1).to_broadcast(ew), ALU.is_gt))
            step(dve.tensor_reduce(extra, cmp[:, :, :], axis=AX_X, op=ALU.add))
            step(dve.tensor_copy(pre[0], extra))
            for n in range(5):
                u, v, d = pre[n % 2], pre[1 - n % 2], 1 << n
                step(dve.tensor_copy(v[:, 0:d], u[:, 0:d]))
                step(dve.tensor_tensor(v[:, d:E], u[:, d:E], u[:, 0:E - d], ALU.add))
            upto = pre[1]
            step(dve.tensor_tensor(before, upto, extra, ALU.subtract))
            tw = [P, QT, OV]
            cmp_t = cmp[:, 0:2, :]
            step(dve.tensor_tensor(cmp_t, rank.unsqueeze(2).to_broadcast(tw), thr.unsqueeze(1).to_broadcast(tw), ALU.is_ge))
            step(dve.tensor_reduce(passes, cmp_t, axis=AX_X, op=ALU.add))
            step(dve.tensor_tensor(logits[:, :, :], onehot[:, :, :], before.unsqueeze(1).to_broadcast(wide), ALU.mult))
            step(dve.tensor_reduce(tile_no, logits[:, :, :], axis=AX_X, op=ALU.add))
            step(dve.scalar_tensor_tensor(tile_no, tile_no, -1.0, passes, ALU.add, ALU.add))
            step(dve.scalar_tensor_tensor(rem, passes, float(-SLOT), rank, ALU.mult, ALU.add))
            step(dve.tensor_scalar(is_more, passes, 1.0, None, ALU.min))
            step(dve.scalar_tensor_tensor(s_first, eidm, float(SLOT), rank, ALU.mult, ALU.add))
            step(dve.tensor_scalar(s_first, s_first, float(SLOT * E), None, ALU.add))
            step(dve.scalar_tensor_tensor(s_more, tile_no, float(SLOT), rem, ALU.mult, ALU.add))
            step(dve.tensor_scalar(s_more, s_more, float(SLOT * E), None, ALU.add))
            step(dve.tensor_tensor(s_more, s_more, s_first, ALU.subtract))
            step(dve.tensor_tensor(s_more, s_more, is_more, ALU.mult))
            step(dve.tensor_tensor(s_first, s_first, s_more, ALU.add))
            for t in range(QT):
                last = dve.tensor_scalar(slot_rep[:, t, :], ones[:, :], s_first[:, t:t + 1], None, ALU.mult)
            last.then_inc(s["slotrep_ready"], 1)
            selection(0)
            dve.wait_ge(s["slotrow_in_psum"], 1)
            dve.tensor_copy(slot_row[:, :], ps[:, 7, 0:NQ]).then_inc(s["slotrow_ready"], 1)
            dve.wait_ge(s["slotrow_ready"], 1)

            def expert(n):
                dve.wait_ge(s["silu_ready"], n + 1)
                dve.wait_ge(s["up_done"], n + 1)
                dve.tensor_tensor(hh[:, :], sg[:, :], ps[:, 1, 0:GW], ALU.mult).then_inc(s["h_ready"], 1)
                dve.tensor_scalar(scat[:, :], slot_row[:, :], slot_tab[:, bass.ds(n, 1)], None, ALU.is_equal
                                  ).then_inc(s["scat_ready"], 1)
                dve.wait_ge(s["down_done"], n + 1)
                dve.tensor_copy(dd[:, :], ps[:, 3, :]).then_inc(s["d_ready"], 1)

            expert(0)
            expert(1)
            selection(1)
            for i in range(IC):
                dve.wait_ge(s["sh_up_in_psum"], i + 1)
                dve.wait_ge(s["sh_silu_ready"], i + 1)
                dve.tensor_tensor(h_t[:, i, :], h_t[:, i, :], ps[:, i % 4, 0:NQ], ALU.mult).then_inc(s["sh_h_ready"], 1)
            cmp_oe = cmp[:, :, :].rearrange("p e r -> p (e r)").rearrange("p (r e) -> p r e", e=E)
            oe = [P, OV, E]
            step(dve.tensor_tensor(cmp_oe, upto.unsqueeze(1).to_broadcast(oe), iota32[:, 0:OV].unsqueeze(2).to_broadcast(oe), ALU.is_le))
            step(dve.tensor_reduce(eo[:, 0:OV], cmp_oe, axis=AX_X, op=ALU.add))
            step(dve.tensor_scalar(eo[:, 0:OV], eo[:, 0:OV], float(E - 1), None, ALU.min))
            step(dve.tensor_copy(eo[:, OV:OV + 1], upto[:, E - 1:E]))
            dve.tensor_copy(eo_i[:, :], eo).then_inc(s["overflow_known"], 1)
            step(dve.tensor_tensor(tsel, iota32[:, 0:OV].unsqueeze(1).to_broadcast(tw), tile_no.unsqueeze(2).to_broadcast(tw), ALU.is_equal))
            step(dve.tensor_tensor(tsel, tsel, is_more.unsqueeze(2).to_broadcast(tw), ALU.mult))
            step(dve.tensor_tensor(rank_hot[:, :, :], iota32[:, :].unsqueeze(1).to_broadcast(wide),
                                   rem.unsqueeze(2).to_broadcast(wide), ALU.is_equal))
            for t in range(QT):
                last = dve.tensor_tensor(gsel_ov[:, t, :, :], tsel[:, t, :].unsqueeze(2).to_broadcast([P, OV, SLOT]),
                                         rank_hot[:, t, :].unsqueeze(1).to_broadcast([P, OV, SLOT]), ALU.mult)
            last.then_inc(s["gsel_ready"], 1)
            with dve.Fori(0, (E - 2) // RING) as g:
                for k in range(RING):
                    expert(g * RING + 2 + k)
            more = dve.value_load(eo_i[0:1, 7:8], min_val=0, max_val=OV)
            with dve.If(more > 0):
                with dve.Fori(0, OV) as o:
                    expert(o + E)
                dve.wait_ge(s["scatter_done"], E + OV)
            dve.wait_ge(s["scatter_done"], E)
            for t in range(QT):
                dve.tensor_tensor(x[:, t, :], x[:, t, :], ps[:, 4 + t, :], ALU.add).then_inc(s["out_ready"], 1)


def kernel(**inputs):
    import numpy as np
    import concourse.bacc as bacc
    from concourse.bass_utils import run_bass_kernel_spmd

    g = {k: np.asarray(v) for k, v in inputs.items()}
    ctx = g["ctx_1024"].reshape(NK, D)

    def cut(b):
        return b.reshape(-1, P).T

    gap = NK // NQ
    near = np.concatenate([ctx[gap // 2 - 1::gap], ctx[gap // 2::gap]])
    arrays = dict(
        x=g["x"], ctx_rows=ctx, ctx_t=ctx.T, sel_t=near.T,
        w_qc_t=g["L0_xattn_Wq_c"].T, w_kc_t=g["L0_xattn_Wk_c"].T, w_vc_t=g["L0_xattn_Wv_c"].T,
        w_vs_t=g["L0_xattn_Wv_s"].T, w_g_t=g["L0_xattn_Wg"].T, w_ks=g["L0_xattn_Wk_s"], w_qs=g["L0_xattn_Wq_s"],
        bias_cols=np.concatenate([cut(g[n]) for n in ("L0_xattn_bq_c", "L0_xattn_bk_c", "L0_xattn_bk_s", "L0_xattn_bq_s",
                                                      "L0_attn_bq", "L0_attn_bk")], axis=1),
        bias_rows=np.concatenate([g[n] for n in ("L0_xattn_bv_c", "L0_xattn_bv_s", "L0_xattn_bg", "L0_attn_bv")]),
        w_q=g["L0_attn_Wq"], w_k=g["L0_attn_Wk"], w_v=g["L0_attn_Wv"], w_o=g["L0_attn_Wo"],
        w_router=g["L0_ffn_gate_w"], s_gate=g["L0_ffn_shared_gate_w"], s_up=g["L0_ffn_shared_up_w"],
        s_down=g["L0_ffn_shared_down_w"], r_gate=g["L0_ffn_routed_gate_w"], r_up=g["L0_ffn_routed_up_w"],
        r_down=g["L0_ffn_routed_down_w"])
    arrays = {k: np.ascontiguousarray(v) for k, v in arrays.items()}

    nc = bacc.Bacc("TRN2", target_bir_lowering=False, num_devices=1)
    aps = {k: nc.dram_tensor(f"in_{k}", v.shape, mybir.dt.from_np(v.dtype), kind="ExternalInput").ap()
           for k, v in arrays.items()}
    aps["out"] = nc.dram_tensor("out", (1, NQ, D), F32, kind="ExternalOutput").ap()
    perceiver_layer(nc, aps)
    result = run_bass_kernel_spmd(nc, [{f"in_{k}": v for k, v in arrays.items()}], core_ids=[0])
    return result.results[0]["out"]
```

```python
import concourse.bass as bass
from concourse import mybir
from contextlib import ExitStack

F32 = mybir.dt.float32
F32R = mybir.dt.float32r
BF16 = mybir.dt.bfloat16
I32 = mybir.dt.int32
ACT = mybir.ActivationFunctionType
ALU = mybir.AluOpType
AX_X = mybir.AxisListType.X

P = 128
D = 512
NQ = 256
NK = 25088
HC = D // P
QT = NQ // P
BLK = 512
NB = NK // BLK
KT = BLK // P
NSEL = 2 * NQ
NH = 16
DK = 64
DA = NH * DK
AC = DA // P
HB = 4
E = 32
FI = 1024
IC = FI // P
GE = 8
SLOT = 32
OV = NQ // SLOT - 1
RING = 3
JG = P // SLOT
GW = FI // JG
XSCALE = float(D) ** -0.5
ASCALE = float(DK) ** -0.5
EPS = 1e-5
LOWEST = -3.0e38
MASKED = -1.0e30
assert NB * BLK == NK and NB % 2 == 1 and (E - 2) % RING == 0 and NSEL == HC * P


class Chain:

    def __init__(self, eng, sem):
        self.eng, self.sem, self.n, self.i, self.per = eng, sem, 0, None, 0

    def __call__(self, ins):
        self.n += 1
        ins.then_inc(self.sem, 1)
        self.eng.wait_ge(self.sem, self.n if self.i is None else self.i * self.per + self.n)

    def enter(self, i, per):
        self.i, self.per, self.mark = i, per, self.n

    def leave(self, trips):
        assert self.n - self.mark == self.per, self.n - self.mark
        self.n, self.i = self.mark + self.per * trips, None


def perceiver_layer(nc, a):
    with ExitStack() as ctx:
        LOW = 16512
        RINGB = 81888
        WB = D * FI * 4 // P

        def at(name, shape, dt, offset):
            return nc.alloc_sbuf_tensor_at(name, shape, dt, offset=offset)

        cursor = [LOW]

        def place(name, shape, dt=F32):
            size = 4 if dt in (F32, F32R, I32) else 2
            for s in shape[1:]:
                size *= s
            t = at(name, shape, dt, cursor[0])
            cursor[0] += (size + 31) // 32 * 32
            assert cursor[0] <= RINGB, (name, cursor[0])
            return t

        ident = place("ident", [P, P])
        identb = place("identb", [P, P], BF16)
        maskb = place("maskb", [P, P], BF16)
        ones = place("ones", [P, P])
        upper = place("upper", [P, P])
        iota32i = place("iota32i", [P, SLOT], I32)
        iota32 = place("iota32", [P, SLOT])
        slot_tab_i = place("slot_tab_i", [P, E + OV], I32)
        slot_tab = place("slot_tab", [P, E + OV])
        x = place("x", [P, QT, D])
        cols = place("cols", [P, 32])
        st = place("st", [P, 100])
        w_router = place("w_router", [P, HC, E])
        small = cursor[0]
        rows = place("rows", [P, 5 * D])
        shared_low = cursor[0]

        acc = place("acc", [P, QT, D])
        pexp = place("pexp", [P, QT, BLK])
        pt_hi = place("pt_hi", [P, QT, KT, P], F32R)
        pt_lo = place("pt_lo", [P, QT, KT, P], F32R)
        q_hi = place("q_hi", [P, HC, NQ], F32R)
        q_lo = place("q_lo", [P, HC, NQ], F32R)
        s2c = place("s2c", [P, QT, D])
        gate2 = place("gate2", [P, QT, D])
        w_gate2 = place("w_gate2", [P, HC, D])
        w_gate1 = at("w_gate1", [P, HC, D], F32, cursor[0] - HC * D * 4)
        acc_t = at("acc_t", [P, HC, NQ], F32, shared_low + 1 * 4096)
        c2s = at("c2s", [P, QT, D], F32, shared_low + 2 * 4096)
        c2s_t = at("c2s_t", [P, HC, NQ], F32, shared_low + 3 * 4096)
        gate = at("gate", [P, QT, D], F32, shared_low + 4 * 4096)

        cursor[0] = shared_low
        an = place("an", [P, QT, D])
        a_t = place("a_t", [P, HC, NQ])
        qpad = place("qpad", [P, AC, 2, NQ])
        k_t = place("k_t", [P, AC, NQ])
        va = place("va", [P, QT, DA])

        cursor[0] = small
        y = place("y", [P, QT, D])
        y_t = place("y_t", [P, HC, NQ])
        gsel = place("gsel", [P, QT, E, SLOT])
        gsel_ov = place("gsel_ov", [P, QT, OV, SLOT])
        xg_all = place("xg_all", [P, HC, (E + OV) * SLOT])
        h_t = place("h_t", [P, IC, NQ])
        slot_row = place("slot_row", [P, NQ])
        xg = place("xg", [P, HC, SLOT])
        sg = place("sg", [P, GW])
        hh = place("hh", [P, GW])
        hh_t = place("hh_t", [P, 2, P])
        dd = place("dd", [P, D])
        scat_at = cursor[0]
        scat = place("scat", [P, NQ])
        slot_rep = at("slot_rep", [P, QT, P], F32, scat_at)
        cmp = at("cmp", [P, E, OV], F32, small + 4096 * 2 + 8192)
        eo_i = place("eo_i", [P, 8], I32)
        logits = place("logits", [P, QT, E])
        onehot = place("onehot", [P, QT, E])
        rank_hot = place("rank_hot", [P, QT, E])
        iota_m = place("iota_m", [P, E])
        counts, extra, before, upto0, upto1 = (place(n, [P, E])[:, :] for n in
                                               ("counts", "extra", "before", "upto0", "upto1"))
        pre = [upto0, upto1]
        thr = place("thr", [P, OV])[:, :]
        eo = place("eo", [P, OV + 1])[:, :]
        tsel = place("tsel", [P, QT, OV])[:, :, :]
        tok = place("tok", [P, 10 * QT])
        maxlog, tscale, eidm, rank, passes, tile_no, rem, is_more, s_first, s_more = (
            tok[:, k * QT:(k + 1) * QT] for k in range(10))

        kb = HC * BLK * 4
        nat = [at(f"nat{k}", [P, KT, D], F32, RINGB + k * kb) for k in range(2)]
        ctt = [at(f"ctt{k}", [P, HC, BLK], F32, RINGB + (2 + k) * kb) for k in range(2)]
        nat_hi = [at(f"nat_hi{k}", [P, KT, D], F32R, RINGB + (4 + k) * kb) for k in range(2)]
        nat_lo = [at(f"nat_lo{k}", [P, KT, D], F32R, RINGB + (6 + k) * kb) for k in range(2)]
        ctt_hi = [at(f"ctt_hi{k}", [P, HC, BLK], F32R, RINGB + (8 + k) * kb) for k in range(2)]
        ctt_lo = [at(f"ctt_lo{k}", [P, HC, BLK], F32R, RINGB + (10 + k) * kb) for k in range(2)]
        o = RINGB + 9 * kb
        xn = at("xn", [P, QT, D], F32, o)
        c_t = at("c_t", [P, HC, NQ], F32, o + 4096)
        o = RINGB + 11 * kb
        qc_t = at("qc_t", [P, HC, NQ], F32, o)
        kc_t = at("kc_t", [P, HC, NQ], F32, o + 4096)
        o = RINGB + 5 * kb
        kq_t = at("kq_t", [P, HC, NQ], F32, o)
        vc = at("vc", [P, QT, D], F32, o + 4096)
        o = RINGB + 7 * kb
        sc2 = at("sc2", [P, 4, NQ], F32, o)
        s2c_t = at("s2c_t", [P, HC, NQ], F32, o + 4096)
        o = RINGB + 4 * kb
        pavg = at("pavg", [P, QT, NQ], F32, o)
        pavg_t = at("pavg_t", [P, QT, NQ], F32, o + 2048)
        bias2 = at("bias2", [P, NQ], F32, o + 4096)
        bqs_rep = at("bqs_rep", [P, HC, P], F32, o + 5120)
        o = RINGB + 12 * kb
        w_qc, w_ks, w_kc, w_qs, w_vc, sel_t = (at(n, [P, HC, D], F32, o + k * kb) for k, n in
                                              enumerate(("w_qc", "w_ks", "w_kc", "w_qs", "w_vc", "sel_t")))
        w_vs = at("w_vs", [P, HC, D], F32, RINGB + 3 * kb)
        w_q = at("w_q", [P, HC, DA], F32, RINGB + 2 * 3 * WB)
        w_k = at("w_k", [P, HC, DA], F32, RINGB + (2 * 3 + 1) * WB)
        w_v = at("w_v", [P, HC, DA], F32, RINGB + (2 * 3 + 2) * WB)
        w_o = at("w_o", [P, AC, D], F32, RINGB + 2 * 3 * WB)
        o_t = at("o_t", [P, AC, NQ], F32, RINGB + (2 * 3 + 1) * WB)
        patt = at("patt", [P, HB, 384], F32, RINGB + (2 * 3 + 1) * WB + 8192)
        patt_t = at("patt_t", [P, 2, 384], F32, RINGB + (2 * 3 + 2) * WB)
        wg = [at(f"wg{k}", [P, HC, FI], F32, RINGB + 3 * k * WB) for k in range(RING)]
        wu = [at(f"wu{k}", [P, HC, FI], F32, RINGB + (3 * k + 1) * WB) for k in range(RING)]
        wd = [at(f"wd{k}", [P, IC, D], F32, RINGB + (3 * k + 2) * WB) for k in range(RING)]

        ps = ctx.enter_context(nc.psum_tensor("ps", [P, 8, 512], F32))

        def bank(k, n=1):
            return ps[:, k, :] if n == 1 else ps[:, k:k + n, :]

        b_qc, b_kc, b_ks, b_qs = cols[:, 0:4], cols[:, 4:8], cols[:, 8:12], cols[:, 12:16]
        b_q, b_k = cols[:, 16:24], cols[:, 24:32]
        r_vc, r_vs, r_g, r_v = rows[:, 0:D], rows[:, D:2 * D], rows[:, 2 * D:3 * D], rows[:, 3 * D:5 * D]

        names = """
        x_loaded cols_loaded rows_loaded wqc_loaded wks_loaded wkc_loaded wqs_loaded wvc_loaded sel_loaded
        wg2_loaded wg1_loaded wvs_loaded nat_loaded0 nat_loaded1 ctt_loaded0 ctt_loaded1 watt_loaded wo_loaded
        gw_loaded0 gw_loaded1 gw_loaded2 uw_loaded0 uw_loaded1 uw_loaded2 dw_loaded0 dw_loaded1 dw_loaded2
        wr_loaded out_stored
        identb_made consts_made pool_step dve_step act_step
        var_ready sd_ready
        xn_ready ct_in_psum ct_lo_ready ct_hi_ready qc_in_psum qc_ready kc_in_psum kc_ready qk_in_psum cb_in_psum
        qhi_ready qlo_ready rep_ready bias2_in_psum bias2_ready kq_in_psum kq_ready vc_in_psum vc_ready
        sc2_in_psum sc2_taken neg2_ready p2_ready pavg_ready pavgt_in_psum pavgt_ready s2ct_in_psum s2ct_ready
        s2c_in_psum s2c_ready gate2_in_psum gate2_ready
        nat_hi_ready nat_lo_ready ctt_hi_ready ctt_lo_ready scores_ready bias_ready exp_ready alpha_ready
        pt_in_psum pt_hi_ready pt_lo_ready pv_in_psum acc_ready
        acct_in_psum acct_ready c2s_in_psum c2s_ready c2st_in_psum c2st_ready gate1_in_psum z_ready
        gate_ready an_ready at_in_psum at_ready qpad_zero qa_in_psum qa_evac_act qa_evac_dve ka_in_psum ka_ready
        va_in_psum va_ready
        as_in_psum abias_ready aexp_ready aprob_ready apt_in_psum apt_ready aot_in_psum aot_ready ao_in_psum
        y_ready yt_in_psum yt_ready logits_in_psum maxlog_ready token_scale_ready onehot_ready ranks_in_psum
        sh_gate_in_psum sh_up_in_psum sh_silu_ready sh_h_ready sh_down_done
        gsel_ready gather_in_psum gather_ready slotrep_ready slotrow_in_psum slotrow_ready
        xg_ready gate_done silu_ready up_done h_ready ht_in_psum ht_ready down_done d_ready scat_ready
        scatter_done overflow_known out_ready
        """.split()
        s = {n: ctx.enter_context(nc.semaphore(n)) for n in names}
        nat_loaded = [s["nat_loaded0"], s["nat_loaded1"]]
        ctt_loaded = [s["ctt_loaded0"], s["ctt_loaded1"]]
        gw_loaded = [s["gw_loaded0"], s["gw_loaded1"], s["gw_loaded2"]]
        uw_loaded = [s["uw_loaded0"], s["uw_loaded1"], s["uw_loaded2"]]
        dw_loaded = [s["dw_loaded0"], s["dw_loaded1"], s["dw_loaded2"]]

        def cell(k, n=1):
            return st[:, k:k + n]

        stats, mv, rstd = cell(0, 12), cell(12, 4), cell(16, 2)
        cb, mrun, nbias, dmax = cell(18, 2), [cell(20, 2), cell(22, 2)], [cell(24, 2), cell(26, 2)], cell(28, 2)
        bmax, alpha, rsum, lrun = cell(30, 2), [cell(32, 2), cell(34, 2)], [cell(36, 2), cell(38, 2)], cell(40, 2)
        lrec, max2, neg2, sum2, rec2 = cell(42, 2), cell(44, 4), cell(48, 4), cell(52, 4), cell(80, 4)
        amax, aneg, asum, arec = ([cell(k + 2 * m, 2) for m in range(HB)] for k in (60, 68, 84, 92))
        var, sd, newt = cell(76, 2), cell(78, 2), cell(58, 2)

        block = ctx.enter_context(nc.Block())

        head_bank = [6, 7, 2, 3]
        places = [1, 2, 0]

        def chunks(w, n=P):
            return w.rearrange("(c p) n -> p c n", p=n)

        @block.sync
        def _(sp):
            sp.dma_start(x[:, :, :], a["x"].rearrange("a (t p) d -> p (a t) d", p=P)).then_inc(s["x_loaded"], 16)
            sp.dma_start(cols[:, :], a["bias_cols"]).then_inc(s["cols_loaded"], 16)
            sp.dma_start(w_router[:, :, :], chunks(a["w_router"])).then_inc(s["wr_loaded"], 16)
            for dst, src, sem in ((w_qc, a["w_qc_t"], s["wqc_loaded"]), (w_kc, a["w_kc_t"], s["wkc_loaded"]),
                                  (w_ks, a["w_ks"], s["wks_loaded"]), (w_qs, a["w_qs"], s["wqs_loaded"])):
                sp.dma_start(dst[:, :, :], chunks(src)).then_inc(sem, 16)
            sp.dma_start(rows[:, :], a["bias_rows"].partition_broadcast(P)).then_inc(s["rows_loaded"], 16)

            def load_block(b, par):
                first = b * BLK
                sp.dma_start(ctt[par][:, :, :], chunks(a["ctx_t"])[:, :, bass.ds(first, BLK)]).then_inc(ctt_loaded[par], 16)
                sp.dma_start(nat[par][:, :, :], a["ctx_rows"][bass.ds(first, BLK), :].rearrange("(t p) d -> p t d", p=P)
                             ).then_inc(nat_loaded[par], 16)

            sp.dma_start(w_vc[:, :, :], chunks(a["w_vc_t"])).then_inc(s["wvc_loaded"], 16)
            sp.dma_start(sel_t[:, :, :], chunks(a["sel_t"])).then_inc(s["sel_loaded"], 16)
            load_block(0, 0)
            sp.dma_start(w_gate2[:, :, :], chunks(a["w_g_t"][D:2 * D, :])).then_inc(s["wg2_loaded"], 16)
            load_block(1, 1)
            def next_block(b, par):
                sp.wait_ge(s["ctt_hi_ready"], b - 1)
                sp.wait_ge(s["ctt_lo_ready"], b - 1)
                sp.wait_ge(s["nat_hi_ready"], b - 1)
                sp.wait_ge(s["nat_lo_ready"], b - 1)
                load_block(b, par)

            next_block(2, 0)
            sp.wait_ge(s["gate2_in_psum"], 1)
            sp.dma_start(w_gate1[:, :, :], chunks(a["w_g_t"][0:D, :])).then_inc(s["wg1_loaded"], 16)
            for b, dst, src in ((3, w_k, "w_k"), (4, w_v, "w_v"), (5, w_q, "w_q")):
                next_block(b, b % 2)
                sp.dma_start(dst[:, :, :], chunks(a[src])).then_inc(s["watt_loaded"], 16)
            with sp.Fori(2, (NB - 3) // 2) as i:
                next_block(i * 2 + 2, 0)
                next_block(i * 2 + 3, 1)
            next_block(NB - 1, 0)
            sp.wait_ge(s["ctt_hi_ready"], NB - 1)
            sp.wait_ge(s["ctt_lo_ready"], NB - 1)
            sp.dma_start(w_vs[:, :, :], chunks(a["w_vs_t"])).then_inc(s["wvs_loaded"], 16)

            def load_expert(k, g, u, d):
                sp.dma_start(wg[k][:, :, :], g).then_inc(gw_loaded[k], 16)
                sp.dma_start(wu[k][:, :, :], u).then_inc(uw_loaded[k], 16)
                sp.dma_start(wd[k][:, :, :], d).then_inc(dw_loaded[k], 16)

            def expert_weights(e):
                return (a["r_gate"][bass.ds(e, 1)].rearrange("a (c p) n -> p (a c) n", p=P),
                        a["r_up"][bass.ds(e, 1)].rearrange("a (c p) n -> p (a c) n", p=P),
                        a["r_down"][bass.ds(e, 1)].rearrange("a (c p) n -> p (a c) n", p=P))

            sp.wait_ge(s["c2s_in_psum"], QT)
            load_expert(0, chunks(a["s_gate"]), chunks(a["s_up"]), chunks(a["s_down"]))
            load_expert(1, *expert_weights(0))
            sp.wait_ge(s["qa_in_psum"], AC)
            sp.dma_start(w_o[:, :, :], chunks(a["w_o"])).then_inc(s["wo_loaded"], 16)
            sp.wait_ge(s["ao_in_psum"], 2)
            load_expert(2, *expert_weights(1))

            def next_expert(e, k, done):
                g, u, d = expert_weights(e)
                sp.wait_ge(s["gate_done"], done)
                sp.dma_start(wg[k][:, :, :], g).then_inc(gw_loaded[k], 16)
                sp.wait_ge(s["up_done"], done)
                sp.dma_start(wu[k][:, :, :], u).then_inc(uw_loaded[k], 16)
                sp.wait_ge(s["down_done"], done)
                sp.dma_start(wd[k][:, :, :], d).then_inc(dw_loaded[k], 16)

            g4, u4, d4 = expert_weights(4)
            next_expert(2, 1, done=1)
            next_expert(3, 2, done=2)
            sp.wait_ge(s["sh_gate_in_psum"], IC)
            sp.dma_start(wg[0][:, :, :], g4).then_inc(gw_loaded[0], 16)
            sp.wait_ge(s["sh_up_in_psum"], IC)
            sp.dma_start(wu[0][:, :, :], u4).then_inc(uw_loaded[0], 16)
            next_expert(5, 1, done=3)
            sp.wait_ge(s["sh_down_done"], 1)
            sp.dma_start(wd[0][:, :, :], d4).then_inc(dw_loaded[0], 16)
            next_expert(6, 2, done=4)
            next_expert(7, 0, done=5)
            with sp.Fori(2, (E - 2) // RING) as g:
                for k in range(RING):
                    next_expert(g * RING + 2 + k, places[k], done=g * RING + k)

            sp.wait_ge(s["overflow_known"], 1)
            more = sp.value_load(eo_i[0:1, 7:8], min_val=0, max_val=OV)
            with sp.If(more > 0):
                with sp.Fori(0, OV) as o:
                    e = sp.value_load(eo_i[0:1, bass.ds(o, 1)], min_val=0, max_val=E - 1)
                    sp.wait_ge(s["down_done"], o + E)
                    g_w, u_w, d_w = expert_weights(e)
                    sp.dma_start(wg[0][:, :, :], g_w).then_inc(gw_loaded[0], 16)
                    sp.dma_start(wu[0][:, :, :], u_w).then_inc(uw_loaded[0], 16)
                    sp.dma_start(wd[0][:, :, :], d_w).then_inc(dw_loaded[0], 16)
            for t in range(QT):
                sp.wait_ge(s["out_ready"], t + 1)
                sp.dma_start(a["out"].rearrange("a (t p) d -> p (a t) d", p=P)[:, t, :], x[:, t, :]).then_inc(s["out_stored"], 16)
            sp.wait_ge(s["out_stored"], 32)

        @block.gpsimd
        def _(pool):
            step = Chain(pool, s["pool_step"])
            step(pool.memset(identb[:, :], 0.0))
            pool.affine_select(out=identb[:, :], in_=identb[:, :], compare_op=ALU.not_equal, fill=1.0, base=0,
                               pattern=[[-1, P]], channel_multiplier=1).then_inc(s["identb_made"], 1)
            step(pool.memset(ident[:, :], 0.0))
            step(pool.affine_select(out=ident[:, :], in_=ident[:, :], compare_op=ALU.not_equal, fill=1.0, base=0,
                                    pattern=[[-1, P]], channel_multiplier=1))
            step(pool.memset(maskb[:, :], 0.0))
            step(pool.affine_select(out=maskb[:, :], in_=maskb[:, :], compare_op=ALU.is_ge, fill=MASKED, base=0,
                                    pattern=[[-1, P]], channel_multiplier=1))
            step(pool.memset(ones[:, :], 1.0))
            step(pool.memset(upper[:, :], 1.0))
            step(pool.affine_select(out=upper[:, :], in_=upper[:, :], compare_op=ALU.is_gt, fill=0.0, base=0,
                                    pattern=[[1, P]], channel_multiplier=-1))
            step(pool.iota(iota32i[:, :], pattern=[[1, SLOT]], base=0, channel_multiplier=0))
            step(pool.tensor_copy(iota32[:, :], iota32i[:, :]))
            for j in range(JG):
                step(pool.iota(slot_tab_i[j * SLOT:(j + 1) * SLOT, :], pattern=[[SLOT, E + OV]], base=0,
                               channel_multiplier=1))
            pool.tensor_copy(slot_tab[:, :], slot_tab_i[:, :]).then_inc(s["consts_made"], 1)
            pool.wait_ge(s["an_ready"], QT)
            pool.wait_ge(s["gate1_in_psum"], QT)
            pool.memset(qpad[:, :, :, :], 0.0).then_inc(s["qpad_zero"], 1)

        @block.tensor
        def _(pe):
            mm = pe.matmul

            def keep_warm(n, k):
                for _ in range(n):
                    mm(ps[:, k, 0:P], identb[:, :], identb[:, :], start=True, stop=True)

            def transposes(src, dst, sem, rows_n=QT, cols_n=HC):
                for t in range(rows_n):
                    for c in range(cols_n):
                        last = pe.transpose(dst[:, c, t * P:(t + 1) * P], src[:, t, c * P:(c + 1) * P], ident[:, :])
                last.then_inc(sem, 1)

            def transpose_tiles(src, ready, sem):
                for t in range(QT):
                    pe.wait_ge(ready, t + 1)
                    for c in range(HC):
                        last = pe.transpose(ps[:, t, c * P:(c + 1) * P], src[:, t, c * P:(c + 1) * P], ident[:, :])
                    last.then_inc(sem, 1)

            def by_chunk(k, n=HC):
                return ps[:, k:k + n // 2, :].rearrange("p b (h n) -> p (b h) n", n=NQ)

            def weight_stationary(out, w, act, n_out, sem, per=False):
                for o in range(n_out):
                    for c in range(HC):
                        last = mm(out[:, o, :], w[:, c, o * P:(o + 1) * P], act[:, c, :], start=(c == 0), stop=(c == HC - 1))
                    if per:
                        last.then_inc(sem, 1)
                if not per:
                    last.then_inc(sem, 1)

            def scores(b, par):
                pe.wait_ge(s["ctt_hi_ready"], b + 1)
                pe.wait_ge(s["ctt_lo_ready"], b + 1)
                for q in range(QT):
                    for c in range(HC):
                        qh, ql = q_hi[:, c, q * P:(q + 1) * P], q_lo[:, c, q * P:(q + 1) * P]
                        o = ps[:, 2 * (1 - par) + q, :]
                        mm(o, qh, ctt_hi[par][:, c, :], start=(c == 0), stop=False)
                        mm(o, qh, ctt_lo[par][:, c, :], start=False, stop=False)
                        last = mm(o, ql, ctt_hi[par][:, c, :], start=False, stop=(c == HC - 1))
                last.then_inc(s["scores_ready"], 1)

            def transpose_probs(b):
                pe.wait_ge(s["exp_ready"], b + 1)
                for q in range(QT):
                    for t in range(KT):
                        last = pe.transpose(ps[:, 4 + q, t * P:(t + 1) * P], pexp[:, q, t * P:(t + 1) * P], ident[:, :])
                last.then_inc(s["pt_in_psum"], 1)

            def products(b, par):
                pe.wait_ge(s["nat_hi_ready"], b + 1)
                pe.wait_ge(s["nat_lo_ready"], b + 1)
                pe.wait_ge(s["pt_hi_ready"], b + 1)
                pe.wait_ge(s["pt_lo_ready"], b + 1)
                pe.wait_ge(s["acc_ready"], b + 1)
                for q in range(QT):
                    for t in range(KT):
                        o = ps[:, 6 + q, :]
                        mm(o, pt_hi[:, q, t, :], nat_hi[par][:, t, :], start=(t == 0), stop=False)
                        mm(o, pt_hi[:, q, t, :], nat_lo[par][:, t, :], start=False, stop=False)
                        last = mm(o, pt_lo[:, q, t, :], nat_hi[par][:, t, :], start=False, stop=(t == KT - 1))
                last.then_inc(s["pv_in_psum"], 1)

            pe.wait_ge(s["identb_made"], 1)
            keep_warm(75, 1)
            pe.wait_ge(s["consts_made"], 1)
            pe.wait_ge(s["xn_ready"], QT)
            transposes(xn, by_chunk(0), s["ct_in_psum"])
            pe.wait_ge(s["ct_lo_ready"], 1)
            pe.wait_ge(s["ct_hi_ready"], 1)
            pe.wait_ge(s["wqc_loaded"], 16)
            weight_stationary(by_chunk(2), w_qc, c_t, HC, s["qc_in_psum"])
            pe.wait_ge(s["wkc_loaded"], 16)
            weight_stationary(by_chunk(4), w_kc, c_t, HC, s["kc_in_psum"])
            pe.wait_ge(s["qc_ready"], 1)
            pe.wait_ge(s["wks_loaded"], 16)
            weight_stationary(by_chunk(6), w_ks, qc_t, HC, s["qk_in_psum"])
            pe.wait_ge(s["cols_loaded"], 16)
            for t in range(QT):
                for c in range(HC):
                    last = mm(ps[:, 0, t:t + 1], qc_t[:, c, t * P:(t + 1) * P], b_ks[:, c:c + 1],
                              start=(c == 0), stop=(c == HC - 1))
            last.then_inc(s["cb_in_psum"], 1)
            pe.wait_ge(s["kc_ready"], 1)
            pe.wait_ge(s["wqs_loaded"], 16)
            weight_stationary(by_chunk(2), w_qs, kc_t, HC, s["kq_in_psum"])
            pe.wait_ge(s["rep_ready"], 1)
            for c in range(HC):
                last = mm(ps[:, 1, 0:NQ], bqs_rep[:, c, :], kc_t[:, c, :], start=(c == 0), stop=(c == HC - 1))
            last.then_inc(s["bias2_in_psum"], 1)
            pe.wait_ge(s["wvc_loaded"], 16)
            for t in range(QT):
                for c in range(HC):
                    last = mm(ps[:, 4 + t, :], c_t[:, c, t * P:(t + 1) * P], w_vc[:, c, :], start=(c == 0), stop=(c == HC - 1))
            last.then_inc(s["vc_in_psum"], 1)
            pe.wait_ge(s["kq_ready"], 1)
            pe.wait_ge(s["bias2_ready"], 1)
            pe.wait_ge(s["qlo_ready"], 1)
            pe.wait_ge(s["sel_loaded"], 16)
            out = by_chunk(0)
            for t in range(NSEL // P):
                for c in range(HC):
                    last = mm(out[:, t, :], sel_t[:, c, t * P:(t + 1) * P], kq_t[:, c, :], start=(c == 0), stop=(c == HC - 1))
            last.then_inc(s["sc2_in_psum"], 1)
            scores(0, 0)
            pe.wait_ge(s["pavg_ready"], 1)
            pe.wait_ge(s["vc_ready"], 1)
            transposes(pavg, ps[:, 4, :].rearrange("p (c n) -> p c n", n=NQ), s["pavgt_in_psum"], QT, QT)
            pe.wait_ge(s["pavgt_ready"], 1)
            out = by_chunk(0)
            for o in range(HC):
                for c in range(QT):
                    last = mm(out[:, o, :], vc[:, c, o * P:(o + 1) * P], pavg_t[:, c, :], start=(c == 0), stop=(c == QT - 1))
            last.then_inc(s["s2ct_in_psum"], 1)
            for t in range(QT):
                for c in range(QT):
                    last = mm(ps[:, 6 + t, :], pavg_t[:, c, t * P:(t + 1) * P], vc[:, c, :], start=(c == 0), stop=(c == QT - 1))
            last.then_inc(s["s2c_in_psum"], 1)
            pe.wait_ge(s["s2ct_ready"], 1)
            pe.wait_ge(s["exp_ready"], 1)
            pe.wait_ge(s["wg2_loaded"], 16)
            for t in range(QT):
                for c in range(HC):
                    last = mm(ps[:, 2 + t, :], s2c_t[:, c, t * P:(t + 1) * P], w_gate2[:, c, :], start=(c == 0), stop=(c == HC - 1))
            last.then_inc(s["gate2_in_psum"], 1)
            transpose_probs(0)

            pe.wait_ge(s["s2c_ready"], 1)
            pe.wait_ge(s["gate2_ready"], 1)
            with pe.Fori(0, (NB - 1) // 2) as i:
                for par in (1, 0):
                    b = i * 2 + (1 if par else 2)
                    scores(b, par)
                    products(b - 1, 1 - par)
                    transpose_probs(b)
            keep_warm(50, 0)
            products(NB - 1, 0)

            keep_warm(34, 0)
            pe.wait_ge(s["acc_ready"], NB + 1)
            transposes(acc, by_chunk(0), s["acct_in_psum"])
            keep_warm(20, 2)
            pe.wait_ge(s["acct_ready"], 2)
            pe.wait_ge(s["wvs_loaded"], 16)
            for t in range(QT):
                for c in range(HC):
                    last = mm(ps[:, 2 + t, :], acc_t[:, c, t * P:(t + 1) * P], w_vs[:, c, :], start=(c == 0), stop=(c == HC - 1))
                last.then_inc(s["c2s_in_psum"], 1)
            for t in range(QT):
                pe.wait_ge(s["c2s_ready"], t + 1)
                for c in range(HC):
                    last = pe.transpose(ps[:, 4 + t, c * P:(c + 1) * P], c2s[:, t, c * P:(c + 1) * P], ident[:, :])
                last.then_inc(s["c2st_in_psum"], 1)
            pe.wait_ge(s["wg1_loaded"], 16)
            for t in range(QT):
                pe.wait_ge(s["c2st_ready"], t + 1)
                for c in range(HC):
                    last = mm(ps[:, 6 + t, :], c2s_t[:, c, t * P:(t + 1) * P], w_gate1[:, c, :], start=(c == 0), stop=(c == HC - 1))
                last.then_inc(s["gate1_in_psum"], 1)

            keep_warm(135, 0)
            transpose_tiles(an, s["an_ready"], s["at_in_psum"])
            keep_warm(20, 2)
            pe.wait_ge(s["at_ready"], 2)
            pe.wait_ge(s["watt_loaded"], 48)
            weight_stationary(by_chunk(2, AC), w_q, a_t, AC, s["qa_in_psum"], per=True)
            k_bank = [6, 6, 7, 7, 0, 0, 1, 1]
            for o in range(AC):
                for c in range(HC):
                    last = mm(ps[:, k_bank[o], (o % 2) * NQ:(o % 2 + 1) * NQ], w_k[:, c, o * P:(o + 1) * P], a_t[:, c, :],
                              start=(c == 0), stop=(c == HC - 1))
                last.then_inc(s["ka_in_psum"], 1)
            pe.wait_ge(s["qa_evac_act"], AC)
            pe.wait_ge(s["qa_evac_dve"], AC)
            for t in range(QT):
                for n in range(2):
                    for c in range(HC):
                        last = mm(ps[:, 2 + 2 * t + n, :], a_t[:, c, t * P:(t + 1) * P], w_v[:, c, n * D:(n + 1) * D],
                                  start=(c == 0), stop=(c == HC - 1))
                    last.then_inc(s["va_in_psum"], 1)

            def head_scores(h):
                c, half, o = h // 2, h % 2, ps[:, head_bank[h % HB], :]
                if h >= HB:
                    pe.wait_ge(s["aexp_ready"], h - HB + 1)
                mm(o[:, 0:P], qpad[:, c, half, 0:P], k_t[:, c, 0:P], start=True, stop=True)
                mm(o[:, P:2 * P], qpad[:, c, half, P:2 * P], k_t[:, c, 0:P], start=True, stop=True)
                mm(o[:, 2 * P:3 * P], qpad[:, c, half, P:2 * P], k_t[:, c, P:2 * P], start=True, stop=False)
                mm(o[:, 2 * P:3 * P], identb[:, :], maskb[:, :], start=False, stop=True).then_inc(s["as_in_psum"], 1)

            def head_transposes(h):
                pe.wait_ge(s["aprob_ready"], h + 1)
                for k in range(3):
                    last = pe.transpose(ps[:, h % 2, k * P:(k + 1) * P], patt[:, h % HB, k * P:(k + 1) * P], ident[:, :])
                last.then_inc(s["apt_in_psum"], 1)

            def head_products(h):
                c, half = h // 2, h % 2
                pe.wait_ge(s["apt_ready"], h + 1)
                if half == 0 and c >= 2:
                    pe.wait_ge(s["aot_ready"], c - 1)
                o = ps[DK * half:DK * (half + 1), 4 + c % 2, :]
                va0, va1 = (va[:, t, h * DK:(h + 1) * DK] for t in range(QT))
                mm(o[:, 0:P], va0, patt_t[:, h % 2, 0:P], start=True, stop=True)
                mm(o[:, P:NQ], va0, patt_t[:, h % 2, P:2 * P], start=True, stop=False)
                last = mm(o[:, P:NQ], va1, patt_t[:, h % 2, 2 * P:3 * P], start=False, stop=True)
                if half:
                    last.then_inc(s["aot_in_psum"], 1)

            pe.wait_ge(s["ka_ready"], AC)
            pe.wait_ge(s["va_ready"], 4)
            for h in range(HB - 1):
                head_scores(h)
            for h in range(NH):
                if h + HB - 1 < NH:
                    head_scores(h + HB - 1)
                head_transposes(h)
                if h:
                    head_products(h - 1)
                if h + HB >= NH:
                    keep_warm(12, 6 + h % 2 if h < NH - 1 else 2)
            head_products(NH - 1)
            keep_warm(10, 6)
            pe.wait_ge(s["aot_ready"], AC)
            pe.wait_ge(s["wo_loaded"], 16)
            for t in range(QT):
                for c in range(AC):
                    last = mm(ps[:, 2 + t, :], o_t[:, c, t * P:(t + 1) * P], w_o[:, c, :], start=(c == 0), stop=(c == AC - 1))
                last.then_inc(s["ao_in_psum"], 1)

            keep_warm(70, 6)
            transpose_tiles(y, s["y_ready"], s["yt_in_psum"])
            keep_warm(19, 7)
            pe.wait_ge(s["yt_ready"], 2)
            pe.wait_ge(s["wr_loaded"], 16)
            for t in range(QT):
                for c in range(HC):
                    last = mm(ps[:, 6, t * E:(t + 1) * E], y_t[:, c, t * P:(t + 1) * P], w_router[:, c, :],
                              start=(c == 0), stop=(c == HC - 1))
                    keep_warm(1, 7)
            last.then_inc(s["logits_in_psum"], 1)
            pe.wait_ge(gw_loaded[0], 16)

            def shared_gate(i):
                for c in range(HC):
                    last = mm(ps[:, i % 4, 0:NQ], wg[0][:, c, i * P:(i + 1) * P], y_t[:, c, :], start=(c == 0), stop=(c == HC - 1))
                last.then_inc(s["sh_gate_in_psum"], 1)

            shared_gate(0)
            pe.wait_ge(s["onehot_ready"], 1)
            mm(ps[:, 6, 64:96], upper[:, :], onehot[:, 0, :], start=True, stop=True)
            mm(ps[:, 6, 96:128], ones[:, :], onehot[:, 0, :], start=True, stop=False)
            mm(ps[:, 6, 96:128], upper[:, :], onehot[:, 1, :], start=False, stop=True)
            mm(ps[:, 6, 128:160], ones[:, :], onehot[:, 0, :], start=True, stop=False)
            mm(ps[:, 6, 128:160], ones[:, :], onehot[:, 1, :], start=False, stop=True).then_inc(s["ranks_in_psum"], 1)
            shared_gate(1)

            def tokens_to_slots(part):
                src_all = gsel_ov if part == E // GE else gsel[:, :, part * GE:(part + 1) * GE, :]
                pe.wait_ge(s["gsel_ready"], part + 1)
                for c in range(HC):
                    for t in range(QT):
                        src = src_all[:, t, :, :].rearrange("p e s -> p (e s)")
                        last = mm(ps[:, c, 0:src.shape[1]], y[:, t, c * P:(c + 1) * P], src, start=(t == 0), stop=(t == QT - 1))
                    last.then_inc(s["gather_in_psum"], 1)
                pe.wait_ge(s["gather_ready"], (part + 1) * HC)

            keep_warm(10, 4)
            pe.wait_ge(s["sh_silu_ready"], 2)
            tokens_to_slots(0)

            def expert(n, k, rnd, first=False, last_one=False):
                pe.wait_ge(s["xg_ready"], n + 1)
                pe.wait_ge(gw_loaded[k], rnd)
                for c in range(HC):
                    for j in range(JG):
                        last = mm(ps[j * SLOT:(j + 1) * SLOT, 0, 0:GW], xg[:, c, :], wg[k][:, c, j * GW:(j + 1) * GW],
                                  start=(c == 0), stop=(c == HC - 1))
                last.then_inc(s["gate_done"], 1)
                pe.wait_ge(uw_loaded[k], rnd)
                for c in range(HC):
                    for j in range(JG):
                        last = mm(ps[j * SLOT:(j + 1) * SLOT, 1, 0:GW], xg[:, c, :], wu[k][:, c, j * GW:(j + 1) * GW],
                                  start=(c == 0), stop=(c == HC - 1))
                last.then_inc(s["up_done"], 1)
                if first:
                    pe.wait_ge(s["slotrep_ready"], 1)
                    for t in range(QT):
                        last = pe.transpose(ps[:, 7, t * P:(t + 1) * P], slot_rep[:, t, :], ident[:, :])
                    last.then_inc(s["slotrow_in_psum"], 1)
                pe.wait_ge(s["h_ready"], n + 1)
                for m in range(2):
                    last = pe.transpose(ps[:, 2, m * P:(m + 1) * P], hh[:, m * P:(m + 1) * P], ident[:, :])
                last.then_inc(s["ht_in_psum"], 1)
                if last_one:
                    keep_warm(48, 6)
                pe.wait_ge(s["ht_ready"], n + 1)
                pe.wait_ge(dw_loaded[k], rnd)
                for m in range(2):
                    for j in range(JG):
                        last = mm(ps[j * SLOT:(j + 1) * SLOT, 3, :], hh_t[:, m, j * SLOT:(j + 1) * SLOT],
                                  wd[k][:, 2 * j + m, :], start=(m == 0), stop=(m == 1))
                last.then_inc(s["down_done"], 1)
                if last_one:
                    keep_warm(20, 6)
                pe.wait_ge(s["d_ready"], n + 1)
                pe.wait_ge(s["scat_ready"], n + 1)
                for t in range(QT):
                    last = mm(ps[:, 4 + t, :], scat[:, t * P:(t + 1) * P], dd[:, :], start=first, stop=True,
                              skip_group_check=True)
                last.then_inc(s["scatter_done"], 1)

            expert(0, 1, 16, first=True)
            expert(1, 2, 16)
            pe.wait_ge(s["h_ready"], 2)
            pe.wait_ge(s["d_ready"], 2)
            pe.wait_ge(s["ht_ready"], 2)
            pe.wait_ge(s["silu_ready"], 2)
            for i in range(2, IC):
                if i >= 6:
                    pe.wait_ge(s["sh_silu_ready"], i - 3)
                shared_gate(i)
            pe.wait_ge(uw_loaded[0], 16)
            for i in range(IC):
                if i < 4:
                    pe.wait_ge(s["sh_silu_ready"], i + 5)
                else:
                    pe.wait_ge(s["sh_h_ready"], i - 3)
                for c in range(HC):
                    last = mm(ps[:, i % 4, 0:NQ], wu[0][:, c, i * P:(i + 1) * P], y_t[:, c, :], start=(c == 0), stop=(c == HC - 1))
                last.then_inc(s["sh_up_in_psum"], 1)
            pe.wait_ge(s["sh_h_ready"], IC)
            expert(2, 1, 32)
            pe.wait_ge(dw_loaded[0], 16)
            for i in range(IC):
                for t in range(QT):
                    last = mm(ps[:, 4 + t, :], h_t[:, i, t * P:(t + 1) * P], wd[0][:, i, :], start=False, stop=True,
                              skip_group_check=True)
            last.then_inc(s["sh_down_done"], 1)
            expert(3, 2, 32)
            expert(4, 0, 32)
            for part in range(1, E // GE):
                tokens_to_slots(part)
            with pe.Fori(1, (E - 2) // RING - 1) as g:
                for k in range(RING):
                    expert(g * RING + 2 + k, places[k], g * 16 + 32)
            for k in range(RING):
                expert(E - RING + k, places[k], 16 * ((E - 2) // RING + 1), last_one=(k == RING - 1))
            pe.wait_ge(s["overflow_known"], 1)
            more = pe.value_load(eo_i[0:1, 7:8], min_val=0, max_val=OV)
            with pe.If(more > 0):
                tokens_to_slots(E // GE)
                with pe.Fori(0, OV) as o:
                    expert(o + E, 0, o * 16 + 16 * ((E - 2) // RING + 2))

        @block.scalar
        def _(act):
            step = Chain(act, s["act_step"])

            def deviation(k):
                act.wait_ge(s["var_ready"], k + 1)
                act.activation(sd, var, ACT.Sqrt).then_inc(s["sd_ready"], 1)

            def columns_hi(b, par, sixteens):
                act.wait_ge(ctt_loaded[par], sixteens)
                act.activation(ctt_hi[par][:, :, :], ctt[par][:, :, :], ACT.Copy).then_inc(s["ctt_hi_ready"], 1)

            def rows_hi(b, par, sixteens):
                act.wait_ge(nat_loaded[par], sixteens)
                act.activation(nat_hi[par][:, :, :], nat[par][:, :, :], ACT.Copy).then_inc(s["nat_hi_ready"], 1)

            def probs_hi(b):
                act.wait_ge(s["pt_in_psum"], b + 1)
                act.activation(pt_hi[:, :, :, :].rearrange("p q t n -> p q (t n)"), bank(4, 2), ACT.Copy
                               ).then_inc(s["pt_hi_ready"], 1)

            def exps(b, par):
                act.wait_ge(s["bias_ready"], b + 1)
                for q in range(QT):
                    last = act.activation(pexp[:, q, :], ps[:, 2 * (1 - par) + q, :], ACT.Exp, bias=nbias[par][:, q:q + 1],
                                          accum_out=rsum[par][:, q:q + 1])
                last.then_inc(s["exp_ready"], 1)
                act.activation(alpha[par], dmax, ACT.Exp).then_inc(s["alpha_ready"], 1)

            def two_blocks(i, last=False):
                for par in (1, 0):
                    b = i * 2 + (1 if par else 2)
                    probs_hi(b - 1)
                    rows_hi(b, par, i * 16 + (16 if par else 32))
                    if par or not last:
                        columns_hi(b + 1, 1 - par, i * 16 + 32)
                    exps(b, par)

            deviation(0)
            act.wait_ge(s["ct_in_psum"], 1)
            act.activation(c_t[:, 2:4, :], ps[:, 1, :].rearrange("p (c n) -> p c n", n=NQ), ACT.Copy).then_inc(s["ct_hi_ready"], 1)
            act.wait_ge(s["cols_loaded"], 16)
            act.wait_ge(s["kc_in_psum"], 1)
            for c in range(HC):
                last = act.activation(kc_t[:, c, :], ps[:, 4 + c // 2, (c % 2) * NQ:(c % 2 + 1) * NQ], ACT.Identity,
                                      bias=b_kc[:, c:c + 1])
            last.then_inc(s["kc_ready"], 1)
            act.wait_ge(s["qk_in_psum"], 1)
            act.activation(q_hi[:, :, :], bank(6, 2).rearrange("p b (h n) -> p (b h) n", n=NQ), ACT.Copy,
                           scale=XSCALE).then_inc(s["qhi_ready"], 1)
            act.wait_ge(s["kq_in_psum"], 1)
            act.activation(kq_t[:, :, :], bank(2, 2).rearrange("p b (h n) -> p (b h) n", n=NQ), ACT.Copy).then_inc(s["kq_ready"], 1)
            columns_hi(0, 0, 16)
            act.wait_ge(s["neg2_ready"], 1)
            for t in range(4):
                last = act.activation(sc2[:, t, :], sc2[:, t, :], ACT.Exp, bias=neg2[:, t:t + 1], scale=XSCALE,
                                      accum_out=sum2[:, t:t + 1])
            last.then_inc(s["p2_ready"], 1)
            act.wait_ge(s["pavgt_in_psum"], 1)
            act.activation(pavg_t[:, :, :], ps[:, 4, :].rearrange("p (c n) -> p c n", n=NQ), ACT.Copy).then_inc(s["pavgt_ready"], 1)
            exps(0, 0)
            act.wait_ge(s["s2c_in_psum"], 1)
            act.activation(s2c[:, :, :], bank(6, 2), ACT.Copy).then_inc(s["s2c_ready"], 1)
            columns_hi(1, 1, 16)
            rows_hi(0, 0, 16)
            with act.Fori(0, (NB - 1) // 2 - 1) as i:
                two_blocks(i)
            two_blocks((NB - 1) // 2 - 1, last=True)
            probs_hi(NB - 1)

            act.wait_ge(s["acct_in_psum"], 1)
            act.activation(acc_t[:, 0:2, :], ps[:, 0, :].rearrange("p (c n) -> p c n", n=NQ), ACT.Copy).then_inc(s["acct_ready"], 1)
            for t in range(QT):
                act.wait_ge(s["c2st_in_psum"], t + 1)
                act.activation(c2s_t[:, :, t * P:(t + 1) * P], ps[:, 4 + t, :].rearrange("p (c n) -> p c n", n=P), ACT.Copy
                               ).then_inc(s["c2st_ready"], 1)
            for t in range(QT):
                act.wait_ge(s["z_ready"], t + 1)
                act.activation(gate[:, t, :], gate[:, t, :], ACT.Sigmoid).then_inc(s["gate_ready"], 1)

            deviation(1)
            act.wait_ge(s["at_in_psum"], 1)
            act.activation(a_t[:, :, 0:P], ps[:, 0, :].rearrange("p (c n) -> p c n", n=P), ACT.Copy).then_inc(s["at_ready"], 1)
            act.wait_ge(s["qpad_zero"], 1)
            for o in range(AC):
                act.wait_ge(s["qa_in_psum"], o // 2 * 2 + 2)
                act.activation(qpad[0:DK, o, 0, :], ps[0:DK, 2 + o // 2, (o % 2) * NQ:(o % 2 + 1) * NQ], ACT.Identity,
                               bias=b_q[0:DK, o:o + 1]).then_inc(s["qa_evac_act"], 1)
                act.activation(qpad[DK:P, o, 1, :], ps[DK:P, 2 + o // 2, (o % 2) * NQ:(o % 2 + 1) * NQ], ACT.Identity,
                               bias=b_q[DK:P, o:o + 1]).then_inc(s["qa_evac_dve"], 1)

            def pair_out(c):
                act.wait_ge(s["aot_in_psum"], c + 1)
                act.activation(o_t[:, c, :], ps[:, 4 + c % 2, 0:NQ], ACT.Copy).then_inc(s["aot_ready"], 1)

            for h in range(NH):
                act.wait_ge(s["abias_ready"], h + 1)
                o, m = ps[:, head_bank[h % HB], :], h % HB
                act.activation(patt[:, m, 0:P], o[:, 0:P], ACT.Exp, bias=aneg[m][:, 0:1], scale=ASCALE,
                               accum_out=asum[m][:, 0:1])
                act.activation(patt[:, m, P:3 * P], o[:, P:3 * P], ACT.Exp, bias=aneg[m][:, 1:2], scale=ASCALE,
                               accum_out=asum[m][:, 1:2]).then_inc(s["aexp_ready"], 1)
                if h >= 1:
                    act.wait_ge(s["apt_in_psum"], h)
                    act.activation(patt_t[:, (h - 1) % 2, :], ps[:, (h - 1) % 2, 0:3 * P], ACT.Copy).then_inc(s["apt_ready"], 1)
                if h >= 4 and h % 2 == 0:
                    pair_out((h - 4) // 2)
            act.wait_ge(s["apt_in_psum"], NH)
            act.activation(patt_t[:, 1, :], ps[:, 1, 0:3 * P], ACT.Copy).then_inc(s["apt_ready"], 1)
            pair_out(AC - 2)
            pair_out(AC - 1)

            deviation(2)
            act.wait_ge(s["yt_in_psum"], 1)
            act.activation(y_t[:, :, 0:P], ps[:, 0, :].rearrange("p (c n) -> p c n", n=P), ACT.Copy).then_inc(s["yt_ready"], 1)
            act.wait_ge(s["maxlog_ready"], 1)
            act.activation(tscale, maxlog, ACT.Sigmoid).then_inc(s["token_scale_ready"], 1)

            def shared_silu(i):
                act.wait_ge(s["sh_gate_in_psum"], i + 1)
                act.activation(h_t[:, i, :], ps[:, i % 4, 0:NQ], ACT.Silu).then_inc(s["sh_silu_ready"], 1)
            def slots_out(part):
                w = OV * SLOT if part == E // GE else GE * SLOT
                for c in range(HC):
                    act.wait_ge(s["gather_in_psum"], part * HC + c + 1)
                    act.activation(xg_all[:, c, part * GE * SLOT:part * GE * SLOT + w], ps[:, c, 0:w], ACT.Copy
                                   ).then_inc(s["gather_ready"], 1)
                act.wait_ge(s["gather_ready"], (part + 1) * HC)

            def gather(n):
                act.activation(xg[:, :, :], xg_all[:, :, bass.ds(n * SLOT, SLOT)], ACT.Copy).then_inc(s["xg_ready"], 1)

            def expert(n, more=True):
                act.wait_ge(s["gate_done"], n + 1)
                act.activation(sg[:, :], ps[:, 0, 0:GW], ACT.Silu).then_inc(s["silu_ready"], 1)
                act.wait_ge(s["ht_in_psum"], n + 1)
                act.activation(hh_t[:, :, :].rearrange("p m n -> p (m n)"), ps[:, 2, 0:2 * P], ACT.Copy).then_inc(s["ht_ready"], 1)
                if more:
                    gather(n + 1)

            for i in range(2):
                shared_silu(i)
            slots_out(0)
            gather(0)
            expert(0)
            expert(1)
            for i in range(2, IC):
                shared_silu(i)
            expert(2)
            expert(3)
            expert(4)
            for part in range(1, E // GE):
                slots_out(part)
            with act.Fori(1, (E - 2) // RING - 1) as g:
                for k in range(RING):
                    expert(g * RING + 2 + k)
            for n in range(E - RING, E):
                expert(n, more=(n < E - 1))
            act.wait_ge(s["overflow_known"], 1)
            more = act.value_load(eo_i[0:1, 7:8], min_val=0, max_val=OV)
            with act.If(more > 0):
                slots_out(E // GE)
                gather(E)
                with act.Fori(0, OV - 1) as o:
                    expert(o + E)
                expert(E + OV - 1, more=False)

        @block.vector
        def _(dve):
            step = Chain(dve, s["dve_step"])

            def row_stats(t):
                step(dve.bn_stats(stats[:, 6 * t:6 * t + 6], x[:, t, :]))
                step(dve.bn_aggr(mv[:, 2 * t:2 * t + 2], stats[:, 6 * t:6 * t + 6]))

            def layernorm(k, dst, ready):
                dve.tensor_scalar(var, mv[:, 1:4:2], EPS, None, ALU.add).then_inc(s["var_ready"], 1)
                dve.wait_ge(s["sd_ready"], k + 1)
                step(dve.reciprocal(rstd, sd))
                step(dve.tensor_tensor(newt, rstd, rstd, ALU.mult))
                step(dve.tensor_tensor(newt, newt, var, ALU.mult))
                step(dve.tensor_scalar(newt, newt, -0.5, 1.5, ALU.mult, ALU.add))
                step(dve.tensor_tensor(rstd, rstd, newt, ALU.mult))
                for t in range(QT):
                    dve.tensor_scalar(dst[:, t, :], x[:, t, :], mv[:, 2 * t:2 * t + 1], rstd[:, t:t + 1],
                                      ALU.subtract, ALU.mult).then_inc(ready, 1)
                dve.wait_ge(ready, QT)

            def columns_lo(b, par):
                dve.wait_ge(s["ctt_hi_ready"], b + 1)
                dve.tensor_tensor(ctt_lo[par][:, :, :], ctt[par][:, :, :], ctt_hi[par][:, :, :].bitcast(F32),
                                  ALU.subtract).then_inc(s["ctt_lo_ready"], 1)

            def rows_lo(b, par):
                dve.wait_ge(s["nat_hi_ready"], b + 1)
                dve.tensor_tensor(nat_lo[par][:, :, :], nat[par][:, :, :], nat_hi[par][:, :, :].bitcast(F32),
                                  ALU.subtract).then_inc(s["nat_lo_ready"], 1)

            def probs_lo(b):
                dve.wait_ge(s["pt_hi_ready"], b + 1)
                dve.tensor_tensor(pt_lo[:, :, :, :].rearrange("p q t n -> p q (t n)"), bank(4, 2),
                                  pt_hi[:, :, :, :].rearrange("p q t n -> p q (t n)").bitcast(F32),
                                  ALU.subtract).then_inc(s["pt_lo_ready"], 1)

            def block_max(b, par):
                dve.wait_ge(s["scores_ready"], b + 1)
                step(dve.reduce_max(bmax, bank(2 * (1 - par), 2), AX_X))
                step(dve.tensor_tensor(bmax, bmax, cb, ALU.add))
                step(dve.tensor_tensor(mrun[par], mrun[1 - par], bmax, ALU.max))
                dve.tensor_tensor(nbias[par], cb, mrun[par], ALU.subtract)
                dve.tensor_tensor(dmax, mrun[1 - par], mrun[par], ALU.subtract).then_inc(s["bias_ready"], 1)

            def accumulate(b, par):
                dve.wait_ge(s["pv_in_psum"], b + 1)
                dve.wait_ge(s["alpha_ready"], b + 1)
                for q in range(QT):
                    dve.scalar_tensor_tensor(acc[:, q, :], acc[:, q, :], alpha[par][:, q:q + 1], ps[:, 6 + q, :],
                                             ALU.mult, ALU.add)
                step(dve.tensor_tensor(lrun, lrun, alpha[par], ALU.mult))
                dve.tensor_tensor(lrun, lrun, rsum[par], ALU.add).then_inc(s["acc_ready"], 1)
                dve.wait_ge(s["acc_ready"], b + 2)

            dve.wait_ge(s["x_loaded"], 16)
            for t in range(QT):
                row_stats(t)
            layernorm(0, xn, s["xn_ready"])
            dve.wait_ge(s["ct_in_psum"], 1)
            dve.tensor_copy(c_t[:, 0:2, :], ps[:, 0, :].rearrange("p (c n) -> p c n", n=NQ)).then_inc(s["ct_lo_ready"], 1)
            dve.wait_ge(s["cols_loaded"], 16)
            dve.wait_ge(s["consts_made"], 1)
            for c in range(HC):
                last = dve.tensor_scalar(bqs_rep[:, c, :], ones[:, :], b_qs[:, c:c + 1], None, ALU.mult)
            last.then_inc(s["rep_ready"], 1)
            dve.wait_ge(s["qc_in_psum"], 1)
            for c in range(HC):
                last = dve.tensor_scalar(qc_t[:, c, :], ps[:, 2 + c // 2, (c % 2) * NQ:(c % 2 + 1) * NQ], b_qc[:, c:c + 1],
                                         None, ALU.add)
            last.then_inc(s["qc_ready"], 1)
            dve.wait_ge(s["qhi_ready"], 1)
            dve.wait_ge(s["cb_in_psum"], 1)
            step(dve.tensor_scalar(cb, ps[:, 0, 0:2], XSCALE, None, ALU.mult))
            dve.scalar_tensor_tensor(q_lo[:, :, :].rearrange("p c n -> p (c n)"), bank(6, 2).rearrange("p b n -> p (b n)"),
                                     XSCALE, q_hi[:, :, :].bitcast(F32).rearrange("p c n -> p (c n)"),
                                     ALU.mult, ALU.subtract).then_inc(s["qlo_ready"], 1)
            dve.wait_ge(s["bias2_in_psum"], 1)
            dve.tensor_copy(bias2[:, :], ps[:, 1, 0:NQ]).then_inc(s["bias2_ready"], 1)
            dve.wait_ge(s["rows_loaded"], 16)
            dve.wait_ge(s["vc_in_psum"], 1)
            for t in range(QT):
                last = dve.tensor_tensor(vc[:, t, :], ps[:, 4 + t, :], r_vc, ALU.add)
            last.then_inc(s["vc_ready"], 1)
            columns_lo(0, 0)
            dve.wait_ge(s["sc2_in_psum"], 1)
            dve.wait_ge(s["bias2_ready"], 1)
            for t in range(4):
                last = dve.tensor_tensor(sc2[:, t, :], ps[:, t // 2, (t % 2) * NQ:(t % 2 + 1) * NQ], bias2[:, :], ALU.add)
            last.then_inc(s["sc2_taken"], 1)
            dve.wait_ge(s["sc2_taken"], 1)
            step(dve.reduce_max(max2, sc2[:, :, :], AX_X))
            dve.tensor_scalar(neg2, max2, -XSCALE, None, ALU.mult).then_inc(s["neg2_ready"], 1)
            dve.wait_ge(s["p2_ready"], 1)
            step(dve.reciprocal(rec2, sum2))
            step(dve.tensor_scalar(rec2, rec2, 0.5, None, ALU.mult))
            for t in range(QT):
                step(dve.tensor_scalar(pavg[:, t, :], sc2[:, 2 + t, :], rec2[:, 2 + t:3 + t], None, ALU.mult))
                last = dve.scalar_tensor_tensor(pavg[:, t, :], sc2[:, t, :], rec2[:, t:t + 1], pavg[:, t, :], ALU.mult, ALU.add)
            last.then_inc(s["pavg_ready"], 1)
            dve.memset(lrun, 0.0)
            step(dve.memset(mrun[1], LOWEST))
            block_max(0, 0)
            dve.wait_ge(s["s2ct_in_psum"], 1)
            dve.tensor_copy(s2c_t[:, :, :], bank(0, 2).rearrange("p b (h n) -> p (b h) n", n=NQ)).then_inc(s["s2ct_ready"], 1)
            dve.memset(acc[:, :, :], 0.0).then_inc(s["acc_ready"], 1)
            dve.wait_ge(s["acc_ready"], 1)

            columns_lo(1, 1)
            rows_lo(0, 0)
            dve.wait_ge(s["gate2_in_psum"], 1)
            for t in range(QT):
                last = dve.tensor_tensor(gate2[:, t, :], ps[:, 2 + t, :], r_g, ALU.add)
            last.then_inc(s["gate2_ready"], 1)

            def two_blocks(i, last=False):
                for par in (1, 0):
                    b = i * 2 + (1 if par else 2)
                    probs_lo(b - 1)
                    rows_lo(b, par)
                    dve.wait_ge(s["alpha_ready"], b)
                    block_max(b, par)
                    if par or not last:
                        columns_lo(b + 1, 1 - par)
                    accumulate(b - 1, 1 - par)

            with dve.Fori(0, (NB - 1) // 2 - 1) as i:
                step.enter(i, 8)
                two_blocks(i)
            step.leave((NB - 1) // 2 - 1)
            two_blocks((NB - 1) // 2 - 1, last=True)
            probs_lo(NB - 1)
            accumulate(NB - 1, 0)

            step(dve.reciprocal(lrec, lrun))
            dve.wait_ge(s["acct_in_psum"], 1)
            dve.tensor_copy(acc_t[:, 2:4, :], ps[:, 1, :].rearrange("p (c n) -> p c n", n=NQ)).then_inc(s["acct_ready"], 1)
            for t in range(QT):
                dve.wait_ge(s["c2s_in_psum"], t + 1)
                dve.scalar_tensor_tensor(c2s[:, t, :], ps[:, 2 + t, :], lrec[:, t:t + 1], r_vs, ALU.mult, ALU.add
                                         ).then_inc(s["c2s_ready"], 1)
            dve.wait_ge(s["c2st_in_psum"], QT)
            step(dve.tensor_tensor(x[:, :, :], x[:, :, :], s2c[:, :, :], ALU.add))
            step(dve.tensor_tensor(c2s[:, :, :], c2s[:, :, :], s2c[:, :, :], ALU.subtract))
            for t in range(QT):
                dve.wait_ge(s["gate1_in_psum"], t + 1)
                dve.tensor_tensor(gate[:, t, :], ps[:, 6 + t, :], gate2[:, t, :], ALU.add).then_inc(s["z_ready"], 1)
            for t in range(QT):
                dve.wait_ge(s["gate_ready"], t + 1)
                step(dve.tensor_tensor(c2s[:, t, :], c2s[:, t, :], gate[:, t, :], ALU.mult))
                step(dve.tensor_tensor(x[:, t, :], x[:, t, :], c2s[:, t, :], ALU.add))
                row_stats(t)

            layernorm(1, an, s["an_ready"])
            dve.wait_ge(s["at_in_psum"], 2)
            dve.tensor_copy(a_t[:, :, P:2 * P], ps[:, 1, :].rearrange("p (c n) -> p c n", n=P)).then_inc(s["at_ready"], 1)
            k_bank = [6, 6, 7, 7, 0, 0, 1, 1]
            for o in range(AC):
                dve.wait_ge(s["ka_in_psum"], o // 2 * 2 + 2)
                dve.tensor_scalar(k_t[:, o, :], ps[:, k_bank[o], (o % 2) * NQ:(o % 2 + 1) * NQ], b_k[:, o:o + 1], None,
                                  ALU.add).then_inc(s["ka_ready"], 1)
            for n in range(4):
                dve.wait_ge(s["va_in_psum"], n + 1)
                dve.tensor_tensor(va[:, n // 2, (n % 2) * D:(n % 2 + 1) * D], ps[:, 2 + n, :], r_v[:, (n % 2) * D:(n % 2 + 1) * D],
                                  ALU.add).then_inc(s["va_ready"], 1)

            def head_max(h):
                m, o = h % HB, ps[:, head_bank[h % HB], :]
                dve.wait_ge(s["as_in_psum"], h + 1)
                dve.reduce_max(amax[m][:, 0:1], o[:, 0:P], AX_X)
                step(dve.reduce_max(amax[m][:, 1:2], o[:, P:3 * P], AX_X))
                dve.tensor_scalar(aneg[m], amax[m], -ASCALE, None, ALU.mult).then_inc(s["abias_ready"], 1)

            def head_norm(h):
                m = h % HB
                dve.wait_ge(s["aexp_ready"], h + 1)
                step(dve.reciprocal(arec[m], asum[m]))
                dve.tensor_scalar(patt[:, m, 0:P], patt[:, m, 0:P], arec[m][:, 0:1], None, ALU.mult)
                dve.tensor_scalar(patt[:, m, P:3 * P], patt[:, m, P:3 * P], arec[m][:, 1:2], None, ALU.mult
                                  ).then_inc(s["aprob_ready"], 1)

            for h in range(HB - 1):
                head_max(h)
            for h in range(NH):
                head_norm(h)
                if h + HB - 1 < NH:
                    head_max(h + HB - 1)
            for t in range(QT):
                dve.wait_ge(s["ao_in_psum"], t + 1)
                step(dve.tensor_tensor(x[:, t, :], x[:, t, :], ps[:, 2 + t, :], ALU.add))
                row_stats(t)

            layernorm(2, y, s["y_ready"])
            dve.wait_ge(s["yt_in_psum"], 2)
            dve.tensor_copy(y_t[:, :, P:2 * P], ps[:, 1, :].rearrange("p (c n) -> p c n", n=P)).then_inc(s["yt_ready"], 1)

            dve.wait_ge(s["logits_in_psum"], 1)
            step(dve.tensor_copy(logits[:, :, :], ps[:, 6, 0:QT * E].rearrange("p (t e) -> p t e", e=E)))
            dve.reduce_max(maxlog, logits[:, :, :], AX_X).then_inc(s["maxlog_ready"], 1)
            dve.wait_ge(s["maxlog_ready"], 1)
            wide = [P, QT, E]
            step(dve.tensor_tensor(onehot[:, :, :], logits[:, :, :], maxlog.unsqueeze(2).to_broadcast(wide), ALU.is_equal))
            step(dve.tensor_scalar(iota_m[:, :], iota32[:, :], float(-E), None, ALU.add))
            step(dve.tensor_tensor(logits[:, :, :], onehot[:, :, :], iota_m[:, :].unsqueeze(1).to_broadcast(wide), ALU.mult))
            step(dve.tensor_reduce(eidm, logits[:, :, :], axis=AX_X, op=ALU.min))
            dve.tensor_tensor(onehot[:, :, :], iota_m[:, :].unsqueeze(1).to_broadcast(wide),
                              eidm.unsqueeze(2).to_broadcast(wide), ALU.is_equal).then_inc(s["onehot_ready"], 1)
            dve.wait_ge(s["token_scale_ready"], 1)
            dve.wait_ge(s["onehot_ready"], 1)
            for t in range(QT):
                step(dve.tensor_scalar(y[:, t, :], y[:, t, :], tscale[:, t:t + 1], None, ALU.mult))
            dve.wait_ge(s["ranks_in_psum"], 1)
            step(dve.tensor_tensor(logits[:, :, :], ps[:, 6, 64:128].rearrange("p (t e) -> p t e", e=E), onehot[:, :, :], ALU.mult))
            step(dve.tensor_reduce(rank, logits[:, :, :], axis=AX_X, op=ALU.add))
            step(dve.tensor_tensor(rank_hot[:, :, :], iota32[:, :].unsqueeze(1).to_broadcast(wide),
                                   rank.unsqueeze(2).to_broadcast(wide), ALU.is_equal))

            def selection(part):
                for t in range(QT):
                    last = dve.tensor_tensor(gsel[:, t, part * GE:(part + 1) * GE, :],
                                             onehot[:, t, part * GE:(part + 1) * GE].unsqueeze(2).to_broadcast([P, GE, SLOT]),
                                             rank_hot[:, t, :].unsqueeze(1).to_broadcast([P, GE, SLOT]), ALU.mult)
                last.then_inc(s["gsel_ready"], 1)

            selection(0)
            step(dve.tensor_scalar(thr, iota32[:, 0:OV], float(SLOT), float(SLOT), ALU.mult, ALU.add))
            ew = [P, E, OV]
            step(dve.tensor_copy(counts, ps[:, 6, 128:160]))
            step(dve.tensor_tensor(cmp[:, :, :], counts.unsqueeze(2).to_broadcast(ew), thr.unsqueeze(1).to_broadcast(ew), ALU.is_gt))
            step(dve.tensor_reduce(extra, cmp[:, :, :], axis=AX_X, op=ALU.add))
            step(dve.tensor_copy(pre[0], extra))
            for n in range(5):
                u, v, d = pre[n % 2], pre[1 - n % 2], 1 << n
                step(dve.tensor_copy(v[:, 0:d], u[:, 0:d]))
                step(dve.tensor_tensor(v[:, d:E], u[:, d:E], u[:, 0:E - d], ALU.add))
            upto = pre[1]
            step(dve.tensor_tensor(before, upto, extra, ALU.subtract))
            tw = [P, QT, OV]
            cmp_t = cmp[:, 0:2, :]
            step(dve.tensor_tensor(cmp_t, rank.unsqueeze(2).to_broadcast(tw), thr.unsqueeze(1).to_broadcast(tw), ALU.is_ge))
            step(dve.tensor_reduce(passes, cmp_t, axis=AX_X, op=ALU.add))
            step(dve.tensor_tensor(logits[:, :, :], onehot[:, :, :], before.unsqueeze(1).to_broadcast(wide), ALU.mult))
            step(dve.tensor_reduce(tile_no, logits[:, :, :], axis=AX_X, op=ALU.add))
            step(dve.scalar_tensor_tensor(tile_no, tile_no, -1.0, passes, ALU.add, ALU.add))
            step(dve.scalar_tensor_tensor(rem, passes, float(-SLOT), rank, ALU.mult, ALU.add))
            step(dve.tensor_scalar(is_more, passes, 1.0, None, ALU.min))
            step(dve.scalar_tensor_tensor(s_first, eidm, float(SLOT), rank, ALU.mult, ALU.add))
            step(dve.tensor_scalar(s_first, s_first, float(SLOT * E), None, ALU.add))
            step(dve.scalar_tensor_tensor(s_more, tile_no, float(SLOT), rem, ALU.mult, ALU.add))
            step(dve.tensor_scalar(s_more, s_more, float(SLOT * E), None, ALU.add))
            step(dve.tensor_tensor(s_more, s_more, s_first, ALU.subtract))
            step(dve.tensor_tensor(s_more, s_more, is_more, ALU.mult))
            step(dve.tensor_tensor(s_first, s_first, s_more, ALU.add))
            for t in range(QT):
                last = dve.tensor_scalar(slot_rep[:, t, :], ones[:, :], s_first[:, t:t + 1], None, ALU.mult)
            last.then_inc(s["slotrep_ready"], 1)
            def expert(n, first=False):
                dve.wait_ge(s["silu_ready"], n + 1)
                dve.wait_ge(s["up_done"], n + 1)
                dve.tensor_tensor(hh[:, :], sg[:, :], ps[:, 1, 0:GW], ALU.mult).then_inc(s["h_ready"], 1)
                if first:
                    dve.wait_ge(s["slotrow_in_psum"], 1)
                    dve.tensor_copy(slot_row[:, :], ps[:, 7, 0:NQ]).then_inc(s["slotrow_ready"], 1)
                    dve.wait_ge(s["slotrow_ready"], 1)
                dve.tensor_scalar(scat[:, :], slot_row[:, :], slot_tab[:, bass.ds(n, 1)], None, ALU.is_equal
                                  ).then_inc(s["scat_ready"], 1)
                dve.wait_ge(s["down_done"], n + 1)
                dve.tensor_copy(dd[:, :], ps[:, 3, :]).then_inc(s["d_ready"], 1)

            expert(0, first=True)
            expert(1)
            for part in range(1, E // GE):
                selection(part)
            for i in range(IC):
                dve.wait_ge(s["sh_up_in_psum"], i + 1)
                dve.wait_ge(s["sh_silu_ready"], i + 1)
                dve.tensor_tensor(h_t[:, i, :], h_t[:, i, :], ps[:, i % 4, 0:NQ], ALU.mult).then_inc(s["sh_h_ready"], 1)
            expert(2)
            cmp_oe = cmp[:, :, :].rearrange("p e r -> p (e r)").rearrange("p (r e) -> p r e", e=E)
            oe = [P, OV, E]
            step(dve.tensor_tensor(cmp_oe, upto.unsqueeze(1).to_broadcast(oe), iota32[:, 0:OV].unsqueeze(2).to_broadcast(oe), ALU.is_le))
            step(dve.tensor_reduce(eo[:, 0:OV], cmp_oe, axis=AX_X, op=ALU.add))
            step(dve.tensor_scalar(eo[:, 0:OV], eo[:, 0:OV], float(E - 1), None, ALU.min))
            step(dve.tensor_copy(eo[:, OV:OV + 1], upto[:, E - 1:E]))
            dve.tensor_copy(eo_i[:, :], eo).then_inc(s["overflow_known"], 1)
            step(dve.tensor_tensor(tsel, iota32[:, 0:OV].unsqueeze(1).to_broadcast(tw), tile_no.unsqueeze(2).to_broadcast(tw), ALU.is_equal))
            step(dve.tensor_tensor(tsel, tsel, is_more.unsqueeze(2).to_broadcast(tw), ALU.mult))
            step(dve.tensor_tensor(rank_hot[:, :, :], iota32[:, :].unsqueeze(1).to_broadcast(wide),
                                   rem.unsqueeze(2).to_broadcast(wide), ALU.is_equal))
            for t in range(QT):
                last = dve.tensor_tensor(gsel_ov[:, t, :, :], tsel[:, t, :].unsqueeze(2).to_broadcast([P, OV, SLOT]),
                                         rank_hot[:, t, :].unsqueeze(1).to_broadcast([P, OV, SLOT]), ALU.mult)
            last.then_inc(s["gsel_ready"], 1)
            expert(3)
            expert(4)
            with dve.Fori(1, (E - 2) // RING) as g:
                for k in range(RING):
                    expert(g * RING + 2 + k)
            more = dve.value_load(eo_i[0:1, 7:8], min_val=0, max_val=OV)
            with dve.If(more > 0):
                with dve.Fori(0, OV) as o:
                    expert(o + E)
                dve.wait_ge(s["scatter_done"], E + OV)
            dve.wait_ge(s["scatter_done"], E)
            for t in range(QT):
                dve.tensor_tensor(x[:, t, :], x[:, t, :], ps[:, 4 + t, :], ALU.add).then_inc(s["out_ready"], 1)


def kernel(**inputs):
    import numpy as np
    import concourse.bacc as bacc
    from concourse.bass_utils import run_bass_kernel_spmd

    g = {k: np.asarray(v) for k, v in inputs.items()}
    ctx = g["ctx_1024"].reshape(NK, D)

    def cut(b):
        return b.reshape(-1, P).T

    gap = NK // NQ
    near = np.concatenate([ctx[gap // 2 - 1::gap], ctx[gap // 2::gap]])
    arrays = dict(
        x=g["x"], ctx_rows=ctx, ctx_t=ctx.T, sel_t=near.T,
        w_qc_t=g["L0_xattn_Wq_c"].T, w_kc_t=g["L0_xattn_Wk_c"].T, w_vc_t=g["L0_xattn_Wv_c"].T,
        w_vs_t=g["L0_xattn_Wv_s"].T, w_g_t=g["L0_xattn_Wg"].T, w_ks=g["L0_xattn_Wk_s"], w_qs=g["L0_xattn_Wq_s"],
        bias_cols=np.concatenate([cut(g[n]) for n in ("L0_xattn_bq_c", "L0_xattn_bk_c", "L0_xattn_bk_s", "L0_xattn_bq_s",
                                                      "L0_attn_bq", "L0_attn_bk")], axis=1),
        bias_rows=np.concatenate([g[n] for n in ("L0_xattn_bv_c", "L0_xattn_bv_s", "L0_xattn_bg", "L0_attn_bv")]),
        w_q=g["L0_attn_Wq"], w_k=g["L0_attn_Wk"], w_v=g["L0_attn_Wv"], w_o=g["L0_attn_Wo"],
        w_router=g["L0_ffn_gate_w"], s_gate=g["L0_ffn_shared_gate_w"], s_up=g["L0_ffn_shared_up_w"],
        s_down=g["L0_ffn_shared_down_w"], r_gate=g["L0_ffn_routed_gate_w"], r_up=g["L0_ffn_routed_up_w"],
        r_down=g["L0_ffn_routed_down_w"])
    arrays = {k: np.ascontiguousarray(v) for k, v in arrays.items()}

    nc = bacc.Bacc("TRN2", target_bir_lowering=False, num_devices=1)
    aps = {k: nc.dram_tensor(f"in_{k}", v.shape, mybir.dt.from_np(v.dtype), kind="ExternalInput").ap()
           for k, v in arrays.items()}
    aps["out"] = nc.dram_tensor("out", (1, NQ, D), F32, kind="ExternalOutput").ap()
    perceiver_layer(nc, aps)
    result = run_bass_kernel_spmd(nc, [{f"in_{k}": v for k, v in arrays.items()}], core_ids=[0])
    return result.results[0]["out"]
```
